# Optimizing a Trainium2 kernel written in Bass

```python
import numpy as np
import jax
import jax.numpy as jnp

def _softmax(x, axis=-1):
    return jax.nn.softmax(x, axis=axis)

def _gelu(x):
    return jax.nn.gelu(x, approximate=True)

def _silu(x):
    return jax.nn.silu(x)

def _sigmoid(x):
    return jax.nn.sigmoid(x)

def _layernorm(x, axis=-1, eps=1e-05):
    m = jnp.mean(x, axis=axis, keepdims=True)
    v = jnp.var(x, axis=axis, keepdims=True)
    return (x - m) / jnp.sqrt(v + eps)

def _scatter_add(tgt, idx, src, axis=0):
    return tgt.at[idx].add(src)

def _segment_sum(src, seg, n):
    return jax.ops.segment_sum(src, seg, n)
kernel_name = 'mk_decoder_postln_d1_seqx_r8_9333dc'

def setup_inputs(seed: int=0):
    np.random.seed(seed)
    _w = jnp.asarray

    def _rec_inputs():
        import jax
        import jax.numpy as jnp
        _rk = jax.random.key(seed)
        x = 0.002226 + 0.9996 * jax.random.normal(jax.random.fold_in(_rk, 1), (1, 1024, 128), jnp.float32)
        _lenS = 1024 - jax.random.randint(jax.random.fold_in(_rk, 7), (1,), 0, max(1, 1024 // 4) + 1, jnp.int32)
        _lenS2 = 6404 - jax.random.randint(jax.random.fold_in(_rk, 8), (1,), 0, max(1, 6404 // 4) + 1, jnp.int32)
        _ctx_1024P = jax.random.normal(jax.random.fold_in(_rk, 11), (1, 16, 128), jnp.float32)
        _ctx_1024c = jax.random.dirichlet(jax.random.fold_in(_rk, 511), 0.3 * jnp.ones((16,), jnp.float32), (1, 6404))
        _ctx_1024t = jnp.einsum('bsk,bkd->bsd', _ctx_1024c, _ctx_1024P)
        _ctx_1024t = _ctx_1024t * jax.lax.rsqrt(jnp.mean(jnp.square(_ctx_1024t)) + 1e-12) * 0.953939
        ctx_1024 = -0.000125008 + 0.999885 * (_ctx_1024t + 0.3 * jax.random.normal(jax.random.fold_in(_rk, 611), (1, 6404, 128), jnp.float32))
        return (x, ctx_1024)
    x, ctx_1024 = _rec_inputs()

    def _L0_attn_setup():
        import jax, jax.numpy as jnp
        import numpy as np
        B, L = (2, 256)
        D_MODEL = 128
        D_STATE = 128
        D_CONV = 4
        EXPAND = 2
        HEADDIM = 64
        D_HALF = D_MODEL // 2
        D_INNER = EXPAND * D_HALF
        NHEADS = D_INNER // HEADDIM
        CONV_DIM = D_INNER + 2 * D_STATE
        D_IN_PROJ = 2 * D_INNER + 2 * D_STATE + NHEADS
        EPS = 1e-05

        def _rmsnorm(x, w):
            return x * jax.lax.rsqrt(jnp.mean(x * x, axis=-1, keepdims=True) + EPS) * w

        def _mamba2(u, in_w, conv_w, conv_b, dt_bias, A_log, D, gnorm_w, outp_w):
            b, l, _ = u.shape
            zxbcdt = u @ in_w.T
            z = zxbcdt[..., :D_INNER]
            xBC = zxbcdt[..., D_INNER:D_INNER + CONV_DIM]
            dt = zxbcdt[..., D_INNER + CONV_DIM:]
            xp = jnp.pad(xBC, ((0, 0), (D_CONV - 1, 0), (0, 0)))
            conv = conv_b + sum((xp[:, k:k + l, :] * conv_w[:, k] for k in range(D_CONV)))
            xBC = jax.nn.silu(conv)
            x = xBC[..., :D_INNER]
            Bm = xBC[..., D_INNER:D_INNER + D_STATE]
            Cm = xBC[..., D_INNER + D_STATE:]
            dt = jax.nn.softplus(dt + dt_bias)
            A = -jnp.exp(A_log)
            xh = x.reshape(b, l, NHEADS, HEADDIM)
            dA = jnp.exp(dt * A)
            dtx = dt[..., None] * xh

            def step(h, inp):
                dA_t, dtx_t, B_t, C_t = inp
                h = dA_t[:, :, None, None] * h + jnp.einsum('bhp,bn->bhpn', dtx_t, B_t)
                return (h, jnp.einsum('bhpn,bn->bhp', h, C_t))
            h0 = jnp.zeros((b, NHEADS, HEADDIM, D_STATE), u.dtype)
            xs = (jnp.moveaxis(dA, 1, 0), jnp.moveaxis(dtx, 1, 0), jnp.moveaxis(Bm, 1, 0), jnp.moveaxis(Cm, 1, 0))
            _, ys = jax.lax.scan(step, h0, xs)
            y = jnp.moveaxis(ys, 0, 1) + xh * D[None, None, :, None]
            y = y.reshape(b, l, D_INNER) * jax.nn.silu(z)
            y = _rmsnorm(y, gnorm_w)
            return y @ outp_w.T

        def _forward(x, norm_w, op_w, op_b, f_in_w, f_conv_w, f_conv_b, f_dt_bias, f_A_log, f_D, f_gnorm_w, f_outp_w, b_in_w, b_conv_w, b_conv_b, b_dt_bias, b_A_log, b_D, b_gnorm_w, b_outp_w):
            xn = _rmsnorm(x, norm_w)
            x_f, x_b = (xn[..., :D_HALF], xn[..., D_HALF:])
            out_f = _mamba2(x_f, f_in_w, f_conv_w, f_conv_b, f_dt_bias, f_A_log, f_D, f_gnorm_w, f_outp_w)
            out_b = jnp.flip(_mamba2(jnp.flip(x_b, 1), b_in_w, b_conv_w, b_conv_b, b_dt_bias, b_A_log, b_D, b_gnorm_w, b_outp_w), 1)
            out = jnp.concatenate([out_f, out_b], axis=-1) @ op_w.T + op_b
            return x + out

        def _mamba_params(key, prefix):
            k = jax.random.split(key, 5)
            return {prefix + 'in_w': jax.random.normal(k[0], (D_IN_PROJ, D_HALF), jnp.float32) * 0.02, prefix + 'conv_w': jax.random.normal(k[1], (CONV_DIM, D_CONV), jnp.float32) * 0.2, prefix + 'conv_b': jnp.zeros((CONV_DIM,), jnp.float32), prefix + 'dt_bias': jax.random.normal(k[2], (NHEADS,), jnp.float32) * 0.1, prefix + 'A_log': jnp.log(jax.random.uniform(k[3], (NHEADS,), jnp.float32, 1.0, 16.0)), prefix + 'D': jnp.ones((NHEADS,), jnp.float32), prefix + 'gnorm_w': jnp.ones((D_INNER,), jnp.float32), prefix + 'outp_w': jax.random.normal(k[4], (D_HALF, D_INNER), jnp.float32) * 0.02}
        key = jax.random.key(seed)
        k = jax.random.split(key, 4)
        inp = {'x': jax.random.normal(k[0], (B, L, D_MODEL), jnp.float32), 'norm_w': jnp.ones((D_MODEL,), jnp.float32), 'op_w': jax.random.normal(k[1], (D_MODEL, D_MODEL), jnp.float32) * 0.02, 'op_b': jnp.zeros((D_MODEL,), jnp.float32)}
        inp.update(_mamba_params(k[2], 'f_'))
        inp.update(_mamba_params(k[3], 'b_'))
        return inp
    _L0_attn_all = _L0_attn_setup()
    _L0_attn_in = {k: v for k, v in _L0_attn_all.items() if k in ('norm_w', 'op_w', 'op_b', 'f_in_w', 'f_conv_w', 'f_conv_b', 'f_dt_bias', 'f_A_log', 'f_D', 'f_gnorm_w', 'f_outp_w', 'b_in_w', 'b_conv_w', 'b_conv_b', 'b_dt_bias', 'b_A_log', 'b_D', 'b_gnorm_w', 'b_outp_w')}
    del _L0_attn_all

    def _L0_xattn_setup():
        import jax, jax.numpy as jnp
        import numpy as np
        B, M, N, DIM, DH, H = (8, 512, 64, 128, 128, 8)
        INNER = DH * H
        EPS = 1e-05

        def _layernorm(x, g, b):
            mu = jnp.mean(x, axis=-1, keepdims=True)
            var = jnp.var(x, axis=-1, keepdims=True)
            return (x - mu) * jax.lax.rsqrt(var + EPS) * g + b
        key = jax.random.key(seed)
        ks = jax.random.split(key, 8)
        sd = 0.02
        return {'x': jax.random.normal(ks[0], (B, M, DIM), jnp.float32), 'latents': jax.random.normal(ks[1], (B, N, DIM), jnp.float32), 'gamma_media': jnp.ones((DIM,), jnp.float32), 'beta_media': jnp.zeros((DIM,), jnp.float32), 'gamma_lat': jnp.ones((DIM,), jnp.float32), 'beta_lat': jnp.zeros((DIM,), jnp.float32), 'Wq': jax.random.normal(ks[2], (DIM, INNER), jnp.float32) * sd, 'bq': jnp.zeros((INNER,), jnp.float32), 'Wkv': jax.random.normal(ks[3], (DIM, 2 * INNER), jnp.float32) * sd, 'bkv': jnp.zeros((2 * INNER,), jnp.float32), 'Wo': jax.random.normal(ks[4], (INNER, DIM), jnp.float32) * sd, 'bo': jnp.zeros((DIM,), jnp.float32)}
    _L0_xattn_all = _L0_xattn_setup()
    _L0_xattn_in = {k: v for k, v in _L0_xattn_all.items() if k in ('gamma_media', 'beta_media', 'gamma_lat', 'beta_lat', 'Wq', 'bq', 'Wkv', 'bkv', 'Wo', 'bo')}
    del _L0_xattn_all

    def _L0_ffn_setup():
        import jax, jax.numpy as jnp
        import numpy as np
        B, S, D, F, E, K = (4, 256, 128, 512, 8, 2)
        FS = 128
        LN_EPS = 1e-05

        def _swiglu(x, gu_w, dn_w):
            gate, up = jnp.split(x @ gu_w, 2, axis=-1)
            gate = jnp.clip(gate, -10.0, 10.0)
            return jax.nn.silu(gate) * up @ dn_w
        key = jax.random.key(seed)
        ks = jax.random.split(key, 6)
        s = 0.02
        return {'x': jax.random.normal(ks[0], (B, S, D), jnp.float32), 'ln_gamma': jnp.ones((D,), jnp.float32), 'ln_beta': jnp.zeros((D,), jnp.float32), 'router_w': jax.random.normal(ks[1], (D, E), jnp.float32) * s, 'gate_up_w': jax.random.normal(ks[2], (E, D, 2 * F), jnp.float32) * s, 'down_w': jax.random.normal(ks[3], (E, F, D), jnp.float32) * s, 'shared_gate_up_w': jax.random.normal(ks[4], (D, 2 * FS), jnp.float32) * s, 'shared_down_w': jax.random.normal(ks[5], (FS, D), jnp.float32) * s}
    _L0_ffn_all = _L0_ffn_setup()
    _L0_ffn_in = {k: v for k, v in _L0_ffn_all.items() if k in ('ln_gamma', 'ln_beta', 'router_w', 'gate_up_w', 'down_w', 'shared_gate_up_w', 'shared_down_w')}
    del _L0_ffn_all
    return {'x': x, 'ctx_1024': ctx_1024, 'L0_attn_norm_w': _L0_attn_in['norm_w'], 'L0_attn_op_w': _L0_attn_in['op_w'], 'L0_attn_op_b': _L0_attn_in['op_b'], 'L0_attn_f_in_w': _L0_attn_in['f_in_w'], 'L0_attn_f_conv_w': _L0_attn_in['f_conv_w'], 'L0_attn_f_conv_b': _L0_attn_in['f_conv_b'], 'L0_attn_f_dt_bias': _L0_attn_in['f_dt_bias'], 'L0_attn_f_A_log': _L0_attn_in['f_A_log'], 'L0_attn_f_D': _L0_attn_in['f_D'], 'L0_attn_f_gnorm_w': _L0_attn_in['f_gnorm_w'], 'L0_attn_f_outp_w': _L0_attn_in['f_outp_w'], 'L0_attn_b_in_w': _L0_attn_in['b_in_w'], 'L0_attn_b_conv_w': _L0_attn_in['b_conv_w'], 'L0_attn_b_conv_b': _L0_attn_in['b_conv_b'], 'L0_attn_b_dt_bias': _L0_attn_in['b_dt_bias'], 'L0_attn_b_A_log': _L0_attn_in['b_A_log'], 'L0_attn_b_D': _L0_attn_in['b_D'], 'L0_attn_b_gnorm_w': _L0_attn_in['b_gnorm_w'], 'L0_attn_b_outp_w': _L0_attn_in['b_outp_w'], 'L0_xattn_gamma_media': _L0_xattn_in['gamma_media'], 'L0_xattn_beta_media': _L0_xattn_in['beta_media'], 'L0_xattn_gamma_lat': _L0_xattn_in['gamma_lat'], 'L0_xattn_beta_lat': _L0_xattn_in['beta_lat'], 'L0_xattn_Wq': _L0_xattn_in['Wq'], 'L0_xattn_bq': _L0_xattn_in['bq'], 'L0_xattn_Wkv': _L0_xattn_in['Wkv'], 'L0_xattn_bkv': _L0_xattn_in['bkv'], 'L0_xattn_Wo': _L0_xattn_in['Wo'], 'L0_xattn_bo': _L0_xattn_in['bo'], 'L0_ffn_ln_gamma': _L0_ffn_in['ln_gamma'], 'L0_ffn_ln_beta': _L0_ffn_in['ln_beta'], 'L0_ffn_router_w': _L0_ffn_in['router_w'], 'L0_ffn_gate_up_w': _L0_ffn_in['gate_up_w'], 'L0_ffn_down_w': _L0_ffn_in['down_w'], 'L0_ffn_shared_gate_up_w': _L0_ffn_in['shared_gate_up_w'], 'L0_ffn_shared_down_w': _L0_ffn_in['shared_down_w']}

def reference(x, ctx_1024, L0_attn_norm_w, L0_attn_op_w, L0_attn_op_b, L0_attn_f_in_w, L0_attn_f_conv_w, L0_attn_f_conv_b, L0_attn_f_dt_bias, L0_attn_f_A_log, L0_attn_f_D, L0_attn_f_gnorm_w, L0_attn_f_outp_w, L0_attn_b_in_w, L0_attn_b_conv_w, L0_attn_b_conv_b, L0_attn_b_dt_bias, L0_attn_b_A_log, L0_attn_b_D, L0_attn_b_gnorm_w, L0_attn_b_outp_w, L0_xattn_gamma_media, L0_xattn_beta_media, L0_xattn_gamma_lat, L0_xattn_beta_lat, L0_xattn_Wq, L0_xattn_bq, L0_xattn_Wkv, L0_xattn_bkv, L0_xattn_Wo, L0_xattn_bo, L0_ffn_ln_gamma, L0_ffn_ln_beta, L0_ffn_router_w, L0_ffn_gate_up_w, L0_ffn_down_w, L0_ffn_shared_gate_up_w, L0_ffn_shared_down_w):
    import jax
    import jax.numpy as jnp

    def _L0_attn_ref(x, norm_w, op_w, op_b, f_in_w, f_conv_w, f_conv_b, f_dt_bias, f_A_log, f_D, f_gnorm_w, f_outp_w, b_in_w, b_conv_w, b_conv_b, b_dt_bias, b_A_log, b_D, b_gnorm_w, b_outp_w):
        import jax, jax.numpy as jnp
        import numpy as np
        B, L = (2, 256)
        D_MODEL = 128
        D_STATE = 128
        D_CONV = 4
        EXPAND = 2
        HEADDIM = 64
        D_HALF = D_MODEL // 2
        D_INNER = EXPAND * D_HALF
        NHEADS = D_INNER // HEADDIM
        CONV_DIM = D_INNER + 2 * D_STATE
        D_IN_PROJ = 2 * D_INNER + 2 * D_STATE + NHEADS
        EPS = 1e-05

        def _rmsnorm(x, w):
            return x * jax.lax.rsqrt(jnp.mean(x * x, axis=-1, keepdims=True) + EPS) * w

        def _mamba2(u, in_w, conv_w, conv_b, dt_bias, A_log, D, gnorm_w, outp_w):
            b, l, _ = u.shape
            zxbcdt = u @ in_w.T
            z = zxbcdt[..., :D_INNER]
            xBC = zxbcdt[..., D_INNER:D_INNER + CONV_DIM]
            dt = zxbcdt[..., D_INNER + CONV_DIM:]
            xp = jnp.pad(xBC, ((0, 0), (D_CONV - 1, 0), (0, 0)))
            conv = conv_b + sum((xp[:, k:k + l, :] * conv_w[:, k] for k in range(D_CONV)))
            xBC = jax.nn.silu(conv)
            x = xBC[..., :D_INNER]
            Bm = xBC[..., D_INNER:D_INNER + D_STATE]
            Cm = xBC[..., D_INNER + D_STATE:]
            dt = jax.nn.softplus(dt + dt_bias)
            A = -jnp.exp(A_log)
            xh = x.reshape(b, l, NHEADS, HEADDIM)
            dA = jnp.exp(dt * A)
            dtx = dt[..., None] * xh

            def step(h, inp):
                dA_t, dtx_t, B_t, C_t = inp
                h = dA_t[:, :, None, None] * h + jnp.einsum('bhp,bn->bhpn', dtx_t, B_t)
                return (h, jnp.einsum('bhpn,bn->bhp', h, C_t))
            h0 = jnp.zeros((b, NHEADS, HEADDIM, D_STATE), u.dtype)
            xs = (jnp.moveaxis(dA, 1, 0), jnp.moveaxis(dtx, 1, 0), jnp.moveaxis(Bm, 1, 0), jnp.moveaxis(Cm, 1, 0))
            _, ys = jax.lax.scan(step, h0, xs)
            y = jnp.moveaxis(ys, 0, 1) + xh * D[None, None, :, None]
            y = y.reshape(b, l, D_INNER) * jax.nn.silu(z)
            y = _rmsnorm(y, gnorm_w)
            return y @ outp_w.T

        def _forward(x, norm_w, op_w, op_b, f_in_w, f_conv_w, f_conv_b, f_dt_bias, f_A_log, f_D, f_gnorm_w, f_outp_w, b_in_w, b_conv_w, b_conv_b, b_dt_bias, b_A_log, b_D, b_gnorm_w, b_outp_w):
            xn = _rmsnorm(x, norm_w)
            x_f, x_b = (xn[..., :D_HALF], xn[..., D_HALF:])
            out_f = _mamba2(x_f, f_in_w, f_conv_w, f_conv_b, f_dt_bias, f_A_log, f_D, f_gnorm_w, f_outp_w)
            out_b = jnp.flip(_mamba2(jnp.flip(x_b, 1), b_in_w, b_conv_w, b_conv_b, b_dt_bias, b_A_log, b_D, b_gnorm_w, b_outp_w), 1)
            out = jnp.concatenate([out_f, out_b], axis=-1) @ op_w.T + op_b
            return x + out

        def _mamba_params(key, prefix):
            k = jax.random.split(key, 5)
            return {prefix + 'in_w': jax.random.normal(k[0], (D_IN_PROJ, D_HALF), jnp.float32) * 0.02, prefix + 'conv_w': jax.random.normal(k[1], (CONV_DIM, D_CONV), jnp.float32) * 0.2, prefix + 'conv_b': jnp.zeros((CONV_DIM,), jnp.float32), prefix + 'dt_bias': jax.random.normal(k[2], (NHEADS,), jnp.float32) * 0.1, prefix + 'A_log': jnp.log(jax.random.uniform(k[3], (NHEADS,), jnp.float32, 1.0, 16.0)), prefix + 'D': jnp.ones((NHEADS,), jnp.float32), prefix + 'gnorm_w': jnp.ones((D_INNER,), jnp.float32), prefix + 'outp_w': jax.random.normal(k[4], (D_HALF, D_INNER), jnp.float32) * 0.02}
        return _forward(x, norm_w, op_w, op_b, f_in_w, f_conv_w, f_conv_b, f_dt_bias, f_A_log, f_D, f_gnorm_w, f_outp_w, b_in_w, b_conv_w, b_conv_b, b_dt_bias, b_A_log, b_D, b_gnorm_w, b_outp_w)

    def _L0_xattn_ref(x, latents, gamma_media, beta_media, gamma_lat, beta_lat, Wq, bq, Wkv, bkv, Wo, bo):
        import jax, jax.numpy as jnp
        import numpy as np
        B, M, N, DIM, DH, H = (8, 512, 64, 128, 128, 8)
        INNER = DH * H
        EPS = 1e-05

        def _layernorm(x, g, b):
            mu = jnp.mean(x, axis=-1, keepdims=True)
            var = jnp.var(x, axis=-1, keepdims=True)
            return (x - mu) * jax.lax.rsqrt(var + EPS) * g + b
        b = x.shape[0]
        xn = _layernorm(x, gamma_media, beta_media)
        ln = _layernorm(latents, gamma_lat, beta_lat)
        q = ln @ Wq + bq
        kv_input = jnp.concatenate([xn, ln], axis=1)
        kv = kv_input @ Wkv + bkv
        k, v = jnp.split(kv, 2, axis=-1)

        def to_heads(t):
            return t.reshape(b, t.shape[1], H, DH).transpose(0, 2, 1, 3)
        q, k, v = (to_heads(q), to_heads(k), to_heads(v))
        q = q * DH ** (-0.5)
        sim = jnp.einsum('bhid,bhjd->bhij', q, k)
        attn = jax.nn.softmax(sim, axis=-1)
        out = jnp.einsum('bhij,bhjd->bhid', attn, v)
        out = out.transpose(0, 2, 1, 3).reshape(b, -1, INNER)
        return out @ Wo + bo

    def _L0_ffn_ref(x, ln_gamma, ln_beta, router_w, gate_up_w, down_w, shared_gate_up_w, shared_down_w):
        import jax, jax.numpy as jnp
        import numpy as np
        B, S, D, F, E, K = (4, 256, 128, 512, 8, 2)
        FS = 128
        LN_EPS = 1e-05

        def _swiglu(x, gu_w, dn_w):
            gate, up = jnp.split(x @ gu_w, 2, axis=-1)
            gate = jnp.clip(gate, -10.0, 10.0)
            return jax.nn.silu(gate) * up @ dn_w
        b, s, d = x.shape
        xf = x.reshape(-1, d)
        mu = jnp.mean(xf, axis=-1, keepdims=True)
        var = jnp.var(xf, axis=-1, keepdims=True)
        xn = (xf - mu) * jax.lax.rsqrt(var + LN_EPS) * ln_gamma + ln_beta
        logits = xn @ router_w
        probs = jax.nn.softmax(logits, axis=-1)
        topv, topi = jax.lax.top_k(probs, K)
        topv = topv / jnp.sum(topv, axis=-1, keepdims=True)
        comb = jnp.sum(jax.nn.one_hot(topi, E, dtype=xn.dtype) * topv[..., None], axis=1)
        out = jnp.zeros_like(xf)
        for e in range(E):
            out = out + comb[:, e:e + 1] * _swiglu(xn, gate_up_w[e], down_w[e])
        out = out + _swiglu(xn, shared_gate_up_w, shared_down_w)
        return out.reshape(b, s, d)
    x = _layernorm(x + _L0_attn_ref(x, L0_attn_norm_w, L0_attn_op_w, L0_attn_op_b, L0_attn_f_in_w, L0_attn_f_conv_w, L0_attn_f_conv_b, L0_attn_f_dt_bias, L0_attn_f_A_log, L0_attn_f_D, L0_attn_f_gnorm_w, L0_attn_f_outp_w, L0_attn_b_in_w, L0_attn_b_conv_w, L0_attn_b_conv_b, L0_attn_b_dt_bias, L0_attn_b_A_log, L0_attn_b_D, L0_attn_b_gnorm_w, L0_attn_b_outp_w), axis=-1)
    x = _layernorm(x + _L0_xattn_ref(ctx_1024, x, L0_xattn_gamma_media, L0_xattn_beta_media, L0_xattn_gamma_lat, L0_xattn_beta_lat, L0_xattn_Wq, L0_xattn_bq, L0_xattn_Wkv, L0_xattn_bkv, L0_xattn_Wo, L0_xattn_bo), axis=-1)
    x = _layernorm(x + _L0_ffn_ref(x, L0_ffn_ln_gamma, L0_ffn_ln_beta, L0_ffn_router_w, L0_ffn_gate_up_w, L0_ffn_down_w, L0_ffn_shared_gate_up_w, L0_ffn_shared_down_w), axis=-1)
    return x

_drawn_inputs = setup_inputs


def setup_inputs(seed=0):
    import zlib

    import numpy as np

    out = dict(_drawn_inputs(seed))
    spreads = {'L0_attn_norm_w': (1.0, 0.6),
     'L0_attn_op_b': (0.0, 0.1),
     'L0_attn_f_conv_b': (0.0, 0.588),
     'L0_attn_f_D': (1.0, 0.6),
     'L0_attn_f_gnorm_w': (1.0, 0.6),
     'L0_attn_b_conv_b': (0.0, 0.693),
     'L0_attn_b_D': (1.0, 0.6),
     'L0_attn_b_gnorm_w': (1.0, 0.6),
     'L0_xattn_gamma_media': (1.0, 0.6),
     'L0_xattn_beta_media': (0.0, 0.78),
     'L0_xattn_gamma_lat': (1.0, 0.6),
     'L0_xattn_beta_lat': (0.0, 0.8),
     'L0_xattn_bq': (0.0, 0.8),
     'L0_xattn_bkv': (0.0, 0.1),
     'L0_xattn_bo': (0.0, 0.1),
     'L0_ffn_ln_gamma': (1.0, 0.6),
     'L0_ffn_ln_beta': (0.0, 0.8)}
    factors = {'L0_attn_f_in_w': 3.524,
     'L0_attn_f_conv_w': 6.738,
     'L0_attn_f_dt_bias': 8.0,
     'L0_attn_f_A_log': 8.0,
     'L0_attn_f_outp_w': 3.644,
     'L0_attn_b_in_w': 3.993,
     'L0_attn_b_conv_w': 6.455,
     'L0_attn_b_dt_bias': 8.0,
     'L0_attn_b_A_log': 8.0,
     'L0_attn_b_outp_w': 3.928,
     'L0_xattn_Wq': 8.0,
     'L0_ffn_router_w': 7.202,
     'L0_ffn_gate_up_w': 6.304,
     'L0_ffn_down_w': 6.32,
     'L0_ffn_shared_gate_up_w': 8.0,
     'L0_ffn_shared_down_w': 8.0}
    for name, (base, spread) in spreads.items():
        noise = np.random.default_rng([zlib.crc32(name.encode()), seed]).standard_normal(out[name].shape)
        drawn = base * np.exp(spread * noise) if base else spread * noise
        out[name] = jnp.asarray(drawn.astype(out[name].dtype))
    for name, factor in factors.items():
        out[name] = (out[name] * factor).astype(out[name].dtype)
    return out
```

```python
import numpy as np
from contextlib import ExitStack

import concourse.bass as bass
from concourse import mybir

F32, F16, U32 = mybir.dt.float32, mybir.dt.float16, mybir.dt.uint32
ACT, ALU, AX = mybir.ActivationFunctionType, mybir.AluOpType, mybir.AxisListType

P = 128
D = 128
T = 1024
TC = T // P
CTX = 6404
CC = CTX // P
LEFT = CTX - CC * P
HD = 64
H = 8
E, F, FS = 8, 512, 128
EPS = 1e-5
NCH = 1 + TC + CC
LAT0, CTX0 = 1, 1 + TC
QB = 512
NBLK = H * T // QB
ZS, AS = 16.0, 64.0
SSC = ZS * AS
LIFT = 8 * float(np.log(2))
XS, WS, HS = 16.0, 64.0, 4.0

STEPS = [[0, 1], [2, 3], [4, 5], [6, 7], [8]] + [[CTX0 + 2 * i, CTX0 + 2 * i + 1] for i in range(CC // 2)]
NS = len(STEPS)
assert NS % 6 == 0
LOOP0, LOOPN = 7, 3
TAIL = LOOP0 + 6 * LOOPN
KB = 15
KB_LEFT, KB_LAT = 12, 13
NU = KB * 4
UNITS_HEAD = [0, 2, 2, 2, 2, 2, 2]
UNITS_TURN = [3, 3, 3, 3, 2, 2]
NPART = 6


def is_latent(chunk):
    return LAT0 <= chunk < CTX0


class Turn:

    def __init__(self, i, k):
        self.i, self.k = i, k


def step_number(j, st):
    return NS * j + 6 * st.i + (LOOP0 + st.k) if isinstance(st, Turn) else NS * j + st


def place_of(st):
    return (LOOP0 + st.k, st.i) if isinstance(st, Turn) else (st, 0)


def early(j, st, n):
    return isinstance(j, int) and j == 0 and isinstance(st, int) and st < n


def after(eng, s, n):
    if not (isinstance(n, int) and n == 0):
        eng.wait_ge(s, n)


def layer(nc, a, out):
    ctx = ExitStack()
    with ctx:
        def sb(name, shape, dt=F32):
            return ctx.enter_context(nc.sbuf_tensor(name, shape, dt))

        sems = {}

        def sem(name):
            sems[name] = ctx.enter_context(nc.semaphore(name))
            return sems[name]

        def carve(arena):
            at = [0]

            def take(shape, dt=F32, p=P):
                n = int(np.prod(shape))
                words = n if dt != F16 else (n + 1) // 2
                v = arena[0:p, at[0]:at[0] + words]
                at[0] += words
                assert at[0] <= arena.shape[1], (at[0], arena.shape)
                if dt != F32:
                    v = v.bitcast(dt)
                if len(shape) > 1:
                    names = "abcde"[:len(shape)]
                    v = v.rearrange(f"p ({' '.join(names)}) -> p {' '.join(names)}",
                                    **{k: s for k, s in zip(names, shape)})
                return v
            return take

        PS = ctx.enter_context(nc.psum_tensor("PS", [P, 8, 512], F32))

        z_arena = sb("z_arena", [P, 4 * NCH * P // 2])
        take = carve(z_arena)
        Zhi, Zlo = take([NCH, P], F16), take([NCH, P], F16)
        ZThi, ZTlo = take([NCH * P], F16), take([NCH * P], F16)
        take = carve(z_arena)
        xfT = take([T])
        xfhi, xflo = take([T], F16), take([T], F16)
        hhi, hlo = take([2, 4, QB], F16), take([2, 4, QB], F16)
        sil, hid = take([2, QB]), take([2, QB])
        gcl = take([2, QB])
        xf = take([TC, D])
        lg, pr, cb, cb2 = (take([TC, E]) for _ in range(4))
        mx8, ix8, ixf = take([TC, 8]), take([TC, 8], U32), take([TC, 8])

        p_arena = sb("p_arena", [P, CC * P])
        take = carve(p_arena)
        ctx_sb = take([CC, P])
        take = carve(p_arena)
        Phi, Plo = take([3, 2 * QB], F16), take([3, 2 * QB], F16)
        P32 = take([2, 2 * QB])
        U_sb = take([2, QB])
        take = carve(p_arena)
        brow = take([H * D])
        bsel = take([3, 2, P])

        a_arena = sb("a_arena", [P, 4 * 4 * QB // 2])
        take = carve(a_arena)
        Wq, Wkv, Wo = take([H * D]), take([2 * H * D]), take([H, D])
        take = carve(a_arena)
        A = take([4, 4, QB], F16)

        w_arena = sb("w_arena", [P, 15744])
        take = carve(w_arena)
        GUhi, GUlo = take([E, 2 * F], F16), take([E, 2 * F], F16)
        DNhi, DNlo = take([E, 4, D], F16), take([E, 4, D], F16)
        SGhi, SGlo = take([2 * FS], F16), take([2 * FS], F16)
        SDhi, SDlo = take([D], F16), take([D], F16)
        stage = take([2, 2 * F + 4 * D])
        take = carve(w_arena)
        x_sb = take([TC, D])
        xT2 = take([2, T + 3])
        iw, iwk = take([2, 4, HD]), take([2, 3, 4, HD])
        WcT, WzT, WdT = take([2, 3, 2, P]), take([2, P]), take([2, 2])
        iwdt = take([2, HD])
        yo = take([2, TC, D + 1])
        ow, opw, opT, Wout = take([P]), take([P]), take([P]), take([2, P])
        zs, xc, Bc, Cc = take([2, P]), take([2, P]), take([2, P]), take([2, P])
        LT, Dec, Mt, CD, dg = (take([2, 2, P]) for _ in range(5))
        Xp, Hp = take([2, 3 * P]), take([2, 3 * P])
        yg, sq = take([2, P]), take([2, P])

        AH = sb("AH", [P, H, 2, D])
        xs2 = AH[:].rearrange("p c q (k d) -> p c q k d", k=2)
        VO = sb("VO", [P, H, 2, D + 2])
        WT = sb("WT", [P, 5 * P])
        A_now = sb("A_now", [P, 2, D])
        acc = sb("acc", [P, TC, D])
        zlT = sb("zlT", [P, T])
        take = carve(zlT)
        Bm, Xw, y1 = take([2, P]), take([2, P]), take([2, P])
        Ht = take([2, 2, HD])
        junk = y1[:, 0, :]
        R0 = sb("R0", [1, 2, QB])
        I32, J32, ones, Epat = (sb(n, [P, P]) for n in ("I32", "J32", "ones", "Epat"))
        I16 = sb("I16", [P, P], F16)
        Tm = sb("Tm", [P, 2, P])
        zer = sb("zer", [P, P])
        vecs = sb("vecs", [P, 64])
        ctxl = sb("ctxl", [LEFT, P])
        opb, boB = sb("opb", [P, D]), sb("boB", [P, D])
        dtb, Alog, Aneg = (sb(n, [P, 2, 2]) for n in ("dtb", "Alog", "Aneg"))
        dtc = sb("dtc", [P, 6, 2, TC, 2])
        st6 = sb("st6", [P, CC + 1, 6])
        mv = sb("mv", [P, CC + 1, 2])
        rs = sb("rs", [P, 4, CC + 1])
        ssx = sb("ssx", [P, TC])
        mxs = sb("mxs", [P, 4, KB])
        mcol = sb("mcol", [P, 2, 4])
        rden = sb("rden", [P, 4])
        iota8 = sb("iota8", [P, E])
        rw = sb("rw", [P, E])
        rt = sb("rt", [P, 6, TC])
        V = {n: vecs[:, i:i + 1] for i, n in enumerate(
            ["nw_f", "nw_b", "g_m", "b_m", "g_l", "b_l", "g_f", "b_f", "gw_f", "gw_b", "D_f", "D_b"])}
        cw = vecs[:, 16:40].rearrange("p (q g k) -> p q g k", q=2, g=3)
        cbias = vecs[:, 40:46].rearrange("p (q g) -> p q g", q=2)

        ld_x, ld_mw, ld_aw, ld_ctx, ld_fv = sem("ld_x"), sem("ld_mw"), sem("ld_aw"), sem("ld_ctx"), sem("ld_fv")
        ld_st = [sem("ld_st0"), sem("ld_st1")]
        stage_used = sem("stage_used")
        consts = sem("consts")
        pool_step, dve_step = sem("pool_step"), sem("dve_step")
        sq_in, sq_out = sem("sq_in"), sem("sq_out")
        ss_x = sem("ss_x")
        xs_ready, xT_ps, xT_a, xT_v = sem("xs_ready"), sem("xT_ps"), sem("xT_a"), sem("xT_v")
        iwk_ready, w_ps, w_sb = sem("iwk_ready"), sem("w_ps"), sem("w_sb")
        op_ps, op_sb = sem("op_ps"), sem("op_sb")
        dt_ps, dt_v, dt_a = sem("dt_ps"), sem("dt_v"), sem("dt_a")
        m_init = sem("m_init")
        two = lambda n: [sem(n + "_f"), sem(n + "_b")]
        conv_done, silu_done, dg_ready, t_done, b1_read = map(two, ("conv", "silu", "dg", "tr", "b1"))
        g_done, dec_ready, cdec_ready, m_done, xw_done = map(two, ("g", "dec", "cdec", "mm", "xw"))
        y_done, y1_done, yg_done, sq_done, out_done = map(two, ("y", "y1", "yg", "sq", "outm"))
        out_evac, s_done, ht_done, h_done = map(two, ("oev", "s", "ht", "h"))
        yo_ready, J_ps = sem("yo_ready"), sem("J_ps")
        zl_ready, zlT_ps, zlT_a, zlT_v = sem("zl_ready"), sem("zlT_ps"), sem("zlT_a"), sem("zlT_v")
        zc_ready, z_scaled, z_ones, z_hi, z_lo = sem("zc_ready"), sem("z_scaled"), sem("z_ones"), sem("z_hi"), sem("z_lo")
        zt_ps, zt_hi, zt_lo = sem("zt_ps"), sem("zt_hi"), sem("zt_lo")
        bsel_ready, ld_b = sem("bsel_ready"), sem("ld_b")
        t_ready, wt_ps, wt_sb, ah_ps, ah_sb = sem("t_ready"), sem("wt_ps"), sem("wt_sb"), sem("ah_ps"), sem("ah_sb")
        a_stage, a_ps, a_hi, a_lo, r0_done = sem("a_stage"), sem("a_ps"), sem("a_hi"), sem("a_lo"), sem("r0_done")
        mx_done, mx_read, m_col, m_neg, m_row = sem("mx_done"), sem("mx_read"), sem("m_col"), sem("m_neg"), sem("m_row")
        row_sum, row_hi, row_lo = sem("row_sum"), sem("row_hi"), sem("row_lo")
        qk_done, hi_ready, p32_ready, lo_ready = sem("qk_done"), sem("hi_ready"), sem("p32_ready"), sem("lo_ready")
        pv_done, u_evac, o_ps, o_rd, o_acc = sem("pv_done"), sem("u_evac"), sem("o_ps"), sem("o_rd"), sem("o_acc")
        w_scaled, w_head = sem("w_scaled"), sem("w_head")
        xf_ready, xfT_ps, xfT_v, xf_hi, xf_lo = sem("xf_ready"), sem("xfT_ps"), sem("xfT_v"), sem("xf_hi"), sem("xf_lo")
        rt_ps, rt_v, rt_a, comb_ready = sem("rt_ps"), sem("rt_v"), sem("rt_a"), sem("comb_ready")
        f_ps, f_clip, f_silu, f_hid, f_hi, f_lo = (sem(n) for n in ("f_ps", "f_clip", "f_silu", "f_hid", "f_hi", "f_lo"))
        dn_ps, dn_acc = sem("dn_ps"), sem("dn_acc")
        fin, stored = sem("fin"), sem("stored")

        block = ctx.enter_context(nc.Block())

        def xp_blocks(t, q):
            return t[:, q].rearrange("p (h n) -> p h n", h=2)[:, :, 0:HD]

        def bcast_row(v, n):
            return v.rearrange("(o d) -> o d", o=1).to_broadcast([n, v.shape[0]])

        def col(v):
            return v.rearrange("(d o) -> d o", o=1)

        def loads(eng, s, pairs):
            for dst, src in pairs:
                eng.dma_start(dst, src).then_inc(s, 16)
            return 16 * len(pairs)

        dirs = [a["f"], a["b"]]
        mw = []
        for q, m in enumerate(dirs):
            lo, hi = HD * q, HD * q + HD
            mw += [(iw[:, q], m["in_w"][0:4 * P, :].rearrange("(g p) d -> p g d", p=P)),
                   (iwdt[0:2, q], m["in_w"][4 * P:4 * P + 2, :]),
                   (cw[:, q], m["conv_w"].rearrange("(g p) k -> p g k", p=P)),
                   *((cbias[:, q, g:g + 1], col(m["conv_b"][g * P:(g + 1) * P])) for g in range(3)),
                   (dtb[:, q], bcast_row(m["dt_bias"], P)), (Alog[:, q], bcast_row(m["A_log"], P)),
                   (V["gw_" + "fb"[q]], col(m["gnorm_w"])),
                   (ow[lo:hi, :], m["outp_w"])]
            mw += [(V["nw_" + "fb"[q]][r:r + HD], col(a["norm_w"][lo:hi])) for r in (0, HD)]
            mw += [(V["D_" + "fb"[q]][HD * h:HD * h + HD], bcast_row(m["D"][h:h + 1], HD)) for h in (0, 1)]
        mw += [(opw, a["op_w"]), (opb[:], bcast_row(a["op_b"], P))]
        N_MW = 16 * len(mw)
        aw = [(V["g_m"], col(a["gamma_media"])), (V["b_m"], col(a["beta_media"])),
              (V["g_l"], col(a["gamma_lat"])), (V["b_l"], col(a["beta_lat"])),
              (Wq, a["Wq"]), (Wkv, a["Wkv"]), (Wo, a["Wo"].rearrange("(h e) n -> e h n", e=D)),
              (boB[:], bcast_row(a["bo"], P))]
        N_AW = 16 * len(aw)
        ct = [(ctx_sb, a["ctx"][0, 0:CC * P, :].rearrange("(p c) d -> p c d", c=CC)),
              (ctxl[:], a["ctx"][0, CC * P:CTX, :])]
        N_CT = 16 * len(ct)
        fv = [(V["g_f"], col(a["ln_gamma"])), (V["b_f"], col(a["ln_beta"])), (rw[:], a["router_w"])]
        N_FV = 16 * len(fv)

        xr = a["x"][0].rearrange("(c p) d -> p c d", p=P)
        outr = out[0].rearrange("(c p) d -> p c d", p=P)

        KV_GROUPS = [(CTX0 + g, min(4, NCH - CTX0 - g)) for g in range(0, CC, 4)]

        def stage_parts(par, dst):
            piece = 256
            at = 0
            for hi, lo in (dst[0:2], dst[2:4]):
                if len(hi.shape) == 3:
                    hi, lo = (x.rearrange("p i d -> p (i d)") for x in (hi, lo))
                for o in range(0, hi.shape[1], piece):
                    w = min(piece, hi.shape[1] - o)
                    yield stage[:, par, at:at + w], hi[:, o:o + w], lo[:, o:o + w]
                    at += w

        @block.sync
        def _(sp):
            sp.dma_start(x_sb, xr).then_inc(ld_x, 16)
            loads(sp, ld_mw, mw)
            loads(sp, ld_ctx, ct)
            loads(sp, ld_aw, aw)
            loads(sp, ld_fv, fv)
            sp.wait_ge(z_lo, len(KV_GROUPS) + 1)
            sp.dma_start(brow[0:1, :], bcast_row(a["bq"], 1)).then_inc(ld_b, 16)
            sp.dma_start(brow[1:3, :], a["bkv"].rearrange("(r n) -> r n", r=2)).then_inc(ld_b, 16)
            sp.wait_ge(zlT_v, 2)
            sp.wait_ge(z_lo, len(KV_GROUPS) + 2)
            for e in range(E + 1):
                if e >= 2:
                    sp.wait_ge(stage_used, NPART * (e - 1))
                b = stage[:, e % 2]
                if e < E:
                    sp.dma_start(b[:, 0:2 * F], a["gate_up_w"][e]).then_inc(ld_st[e % 2], 16)
                    sp.dma_start(b[:, 2 * F:].rearrange("p (i d) -> p i d", i=4),
                                 a["down_w"][e].rearrange("(i p) d -> p i d", p=P)).then_inc(ld_st[e % 2], 16)
                else:
                    sp.dma_start(b[:, 0:2 * FS], a["shared_gate_up_w"]).then_inc(ld_st[e % 2], 16)
                    sp.dma_start(b[:, 2 * FS:2 * FS + D], a["shared_down_w"]).then_inc(ld_st[e % 2], 16)
            for c in range(TC):
                sp.wait_ge(fin, c + 1)
                sp.dma_start(outr[:, c, :], xf[:, c, :]).then_inc(stored, 16)
            sp.wait_ge(stored, 16 * TC)

        @block.gpsimd
        def _(pool):
            g = nc.gpsimd
            n = [0]

            def settle(ins):
                n[0] += 1
                ins.then_inc(pool_step, 1)
                pool.wait_ge(pool_step, n[0])

            g.memset(J32[:], 0.0)
            g.memset(ones[:], 1.0)
            g.memset(zer[:], 0.0)
            settle(g.memset(I32[:], 0.0))
            g.iota(iota8[:], [[1, E]], base=0, channel_multiplier=0, allow_small_or_imprecise_dtypes=True)
            g.affine_select(out=J32[:], in_=J32[:], compare_op=ALU.not_equal, fill=1.0, base=1 - P,
                            pattern=[[1, P]], channel_multiplier=1)
            settle(g.affine_select(out=I32[:], in_=I32[:], compare_op=ALU.not_equal, fill=1.0, base=0,
                                   pattern=[[-1, P]], channel_multiplier=1))
            g.tensor_copy(I16[:], I32[:])
            settle(g.tensor_copy(Epat[:], I32[:]))
            g.memset(Epat[0:1, 1:P], -1.0)
            g.memset(Xp.rearrange("p q n -> p (q n)"), 0.0)
            g.memset(Hp.rearrange("p q n -> p (q n)"), 0.0)
            g.memset(xT2.rearrange("p q n -> p (q n)"), 0.0)
            g.memset(Zhi[:, 0, :], 0.0)
            g.memset(Zlo[:, 0, :], 0.0)
            g.memset(ZThi[:, 0:P], 0.0)
            g.memset(ZTlo[:, 0:P], 0.0)
            g.memset(VO[:], 0.0).then_inc(consts, 1)

            pool.wait_ge(ld_mw, N_MW)
            for q in range(2):
                for r in range(3):
                    last = g.tensor_tensor(iwk[:, q, r], iw[:, q, 1 + r].unsqueeze(1).to_broadcast([P, 4, HD]),
                                           cw[:, q, r].unsqueeze(2).to_broadcast([P, 4, HD]), ALU.mult)
            last.then_inc(iwk_ready, 1)

            pool.wait_ge(z_scaled, CC + 1)
            g.memset(ctx_sb[:, :, 0:1], ZS)
            settle(g.memset(ctxl[:, 0:1], ZS))
            for c0, w in KV_GROUPS:
                g.tensor_copy(Zhi[:, c0:c0 + w, :], ctx_sb[:, c0 - CTX0:c0 - CTX0 + w, :]).then_inc(z_hi, 1)
            g.tensor_copy(Zhi[0:LEFT, 0, :], ctxl[:]).then_inc(z_hi, 1)
            for i, (c0, w) in enumerate(KV_GROUPS):
                pool.wait_ge(z_hi, i + 1)
                g.tensor_tensor(Zlo[:, c0:c0 + w, :], ctx_sb[:, c0 - CTX0:c0 - CTX0 + w, :], Zhi[:, c0:c0 + w, :],
                                ALU.subtract).then_inc(z_lo, 1)
            pool.wait_ge(z_hi, len(KV_GROUPS) + 1)
            g.tensor_tensor(Zlo[0:LEFT, 0, :], ctxl[:], Zhi[0:LEFT, 0, :], ALU.subtract).then_inc(z_lo, 1)

            pool.wait_ge(z_lo, len(KV_GROUPS) + 1)
            settle(g.memset(bsel.rearrange("p r g n -> p (r g n)"), 0.0))
            for r in range(3):
                last = g.tensor_copy(bsel[:, r, :, 0:1], I32[:, r:r + 1].unsqueeze(1).to_broadcast([P, 2, 1]))
            last.then_inc(bsel_ready, 1)

            pool.wait_ge(dt_a, 4)
            def diagonals(q, c):
                g.tensor_tensor(dg[:, q], I32[:].unsqueeze(1).to_broadcast([P, 2, P]),
                                dtc[:, 5, q, c, :].unsqueeze(2).to_broadcast([P, 2, P]),
                                ALU.mult).then_inc(dg_ready[q], 1)

            def chunk_pool(c, last=False):
                for q in range(2):
                    pool.wait_ge(dec_ready[q], c + 1)
                    pool.wait_ge(silu_done[q], 4 * c + 4)
                    after(pool, y_done[q], c)
                    g.tensor_tensor(CD[:, q], Dec[:, q], Cc[:, q].unsqueeze(1).to_broadcast([P, 2, P]),
                                    ALU.mult).then_inc(cdec_ready[q], 1)
                for q in range(2):
                    after(pool, out_done[q], c)
                    pool.wait_ge(yg_done[q], c + 1)
                    g.tensor_tensor(sq[:, q], yg[:, q], yg[:, q], ALU.mult).then_inc(sq_done[q], 1)
                    if not last:
                        diagonals(q, c + 1)

            for q in range(2):
                diagonals(q, 0)
            chunk_pool(0)
            with pool.Fori(1, TC - 1) as c:
                chunk_pool(c)
            chunk_pool(TC - 1, last=True)

            pool.wait_ge(zl_ready, 1)
            settle(g.memset(x_sb[:, :, 0:1], ZS))
            g.tensor_copy(Zhi[:, LAT0:CTX0, :], x_sb).then_inc(z_hi, 1)
            pool.wait_ge(z_hi, len(KV_GROUPS) + 2)
            g.tensor_tensor(Zlo[:, LAT0:CTX0, :], x_sb, Zhi[:, LAT0:CTX0, :], ALU.subtract).then_inc(z_lo, 1)

            for e in range(E + 1):
                pool.wait_ge(ld_st[e % 2], 32 * (e // 2) + 32)
                pairs = (GUhi[:, e], GUlo[:, e], DNhi[:, e], DNlo[:, e]) if e < E else (SGhi, SGlo, SDhi, SDlo)
                for k, (src, hi, lo) in enumerate(stage_parts(e % 2, pairs)):
                    n_piece = NPART * e + k + 1
                    g.tensor_scalar(src, src, WS, 0.0, ALU.mult, ALU.add).then_inc(w_scaled, 1)
                    pool.wait_ge(w_scaled, n_piece)
                    g.tensor_copy(hi, src).then_inc(w_head, 1)
                    pool.wait_ge(w_head, n_piece)
                    g.tensor_tensor(lo, src, hi, ALU.subtract).then_inc(stage_used, 1)

        @block.scalar
        def _(act):
            s = nc.scalar

            def root(k):
                act.wait_ge(sq_in, k)
                s.activation(rs[:, 1, :], rs[:, 0, :], ACT.Sqrt).then_inc(sq_out, 1)

            act.wait_ge(ld_x, 16)
            for c in range(TC):
                if c:
                    act.wait_ge(ss_x, c)
                s.activation(junk, x_sb[:, c, :], ACT.Square, accum_out=ssx[:, c:c + 1]).then_inc(ss_x, 1)
            root(1)
            act.wait_ge(xT_ps, 2 * TC)
            act.wait_ge(consts, 1)
            for q in range(2):
                s.copy(xT2[0:HD, q, 3:3 + T].rearrange("p (b n) -> p b n", b=2),
                       PS[0:HD, 2 * q:2 * q + 2, :]).then_inc(xT_a, 1)
            root(2)
            act.wait_ge(zc_ready, 1)
            for c in range(CC):
                s.activation(ctx_sb[:, c, :], ctx_sb[:, c, :], ACT.Identity, bias=rs[:, 2, c:c + 1],
                             scale=rs[:, 3, c:c + 1]).then_inc(z_scaled, 1)
            s.activation(ctxl[:], ctxl[:], ACT.Identity, bias=rs[0:LEFT, 2, CC:CC + 1],
                         scale=rs[0:LEFT, 3, CC:CC + 1]).then_inc(z_scaled, 1)
            for i, (c0, w) in enumerate(KV_GROUPS + [(0, 1)]):
                act.wait_ge(zt_ps, 2 * i + 1)
                n = w * P if c0 else LEFT
                s.copy(ZThi[:, c0 * P:c0 * P + n], PS[:, 4 + 2 * (i % 2), 0:n]).then_inc(zt_hi, 1)
            act.wait_ge(dt_v, 1)
            s.activation(dtc[:, 1], dtc[:, 1], ACT.Exp).then_inc(dt_a, 1)
            s.activation(Aneg[:], Alog[:], ACT.Exp).then_inc(dt_a, 1)
            act.wait_ge(dt_v, 2)
            s.activation(dtc[:, 3], dtc[:, 2], ACT.Ln).then_inc(dt_a, 1)
            act.wait_ge(dt_v, 5)
            s.activation(dtc[:, 5], dtc[:, 4], ACT.Exp).then_inc(dt_a, 1)
            s.activation(rt[:, 5, 0:1], iota8[:, 0:1], ACT.Silu)
            def chunk_act(c):
                for q in range(2):
                    act.wait_ge(conv_done[q], c + 1)
                    after(act, yg_done[q], c)
                    s.activation(zs[:, q], PS[:, 4 * q, 0:P], ACT.Silu).then_inc(silu_done[q], 1)
                    for r, t in enumerate((xc, Bc, Cc)):
                        s.activation(t[:, q], PS[:, 4 * q, (r + 1) * P:(r + 2) * P], ACT.Silu,
                                     bias=cbias[:, q, r:r + 1]).then_inc(silu_done[q], 1)
                for q in range(2):
                    act.wait_ge(out_done[q], c + 1)
                    at = c if q == 0 else (TC - 1) - c
                    s.copy(yo[:, q, at, :], PS[:, 4 * q + 3, P:2 * P + 1]).then_inc(out_evac[q], 1)

            chunk_act(0)
            with act.Fori(1, TC) as c:
                chunk_act(c)
            root(3)
            root(4)
            root(5)
            for h in range(H):
                act.wait_ge(wt_ps, 2 * h + 1)
                if h:
                    act.wait_ge(ah_ps, h)
                s.copy(WT[:, 0:3 * P], PS[:, 2, 0:3 * P]).then_inc(wt_sb, 1)
                act.wait_ge(wt_ps, 2 * h + 2)
                s.copy(WT[:, 3 * P:5 * P], PS[:, 3, 0:2 * P]).then_inc(wt_sb, 1)
                act.wait_ge(ah_ps, h + 1)
                s.activation(AH[:, h], PS[:, 4, 0:2 * P].rearrange("p (g d) -> p g d", g=2), ACT.Copy,
                             scale=AS / ZS * float(D) ** -0.5).then_inc(ah_sb, 1)
                s.copy(VO[:, h, :, 0:D], PS[:, 5, 0:2 * P].rearrange("p (g d) -> p g d", g=2)).then_inc(ah_sb, 1)

            for i in range(2):
                act.wait_ge(zlT_ps, 4 * i + 4)
                s.copy(zlT[:, i * QB:(i + 1) * QB], PS[:, i, :]).then_inc(zlT_a, 1)
                s.copy(ZThi[:, LAT0 * P + i * QB:LAT0 * P + (i + 1) * QB], PS[:, i, :]).then_inc(zlT_a, 1)

            def a_high(b):
                for g in range(2):
                    act.wait_ge(a_ps, 2 * b + g + 1)
                    s.copy(A[:, b % 4, 2 * g, :], PS[:, 7 - g, :]).then_inc(a_hi, 1)

            def weights(j, st):
                g, (r, _) = step_number(j, st), place_of(st)
                w = len(STEPS[r]) * QB
                ps = PS[:, 2 * (r % 2):2 * (r % 2) + 2, :].rearrange("p b n -> p (b n)")[:, 0:w]
                act.wait_ge(qk_done, g + 1)
                if not early(j, st, 3):
                    act.wait_ge(pv_done, g - 2)
                s.activation(Phi[:, r % 3, 0:w], ps, ACT.Exp, scale=1 / SSC).then_inc(hi_ready, 1)
                if not early(j, st, 2):
                    act.wait_ge(lo_ready, g - 1)
                s.activation(P32[:, r % 2, 0:w], ps, ACT.Exp, scale=1 / SSC).then_inc(p32_ready, 1)

            def evac(j):
                act.wait_ge(pv_done, NS * j + NS)
                if not (isinstance(j, int) and j == 0):
                    act.wait_ge(o_ps, 2 * j)
                s.copy(U_sb, PS[:, 4:6, :]).then_inc(u_evac, 1)

            def block_act(j, first=False, nxt=True):
                for st in range(LOOP0):
                    weights(j, st)
                    if st == 1 and not first:
                        evac(j - 1)
                with act.Fori(0, LOOPN) as i:
                    for k in range(6):
                        weights(j, Turn(i, k))
                for st in range(TAIL, NS):
                    weights(j, st)
                    if st == NS - 2 and nxt:
                        a_high(j + 2)

            a_high(0)
            a_high(1)
            s.activation(rt[:, 5, 0:1], iota8[:, 0:1], ACT.Exp)
            block_act(0, first=True)
            with act.Fori(1, NBLK - 2) as j:
                block_act(j)
            block_act(NBLK - 2, nxt=False)
            block_act(NBLK - 1, nxt=False)
            evac(NBLK - 1)

            root(6)
            root(7)
            act.wait_ge(xfT_v, 2)
            s.activation(xfhi, xfT, ACT.Copy, scale=XS).then_inc(xf_hi, 1)
            act.wait_ge(rt_v, 1)
            for c in range(TC):
                s.activation(pr[:, c], lg[:, c], ACT.Exp, bias=rt[:, 0, c:c + 1],
                             accum_out=rt[:, 1, c:c + 1]).then_inc(rt_a, 1)
            s.activation(rt[:, 5, 0:1], iota8[:, 0:1], ACT.Silu)

            def silu(u, k):
                act.wait_ge(f_clip, u + 1)
                if not (isinstance(u, int) and u < 2):
                    act.wait_ge(f_hid, u - 1)
                s.activation(sil[:, k % 2], gcl[:, k % 2], ACT.Silu, scale=1 / (XS * WS)).then_inc(f_silu, 1)

            def high(u, k, g2, i, first):
                act.wait_ge(f_hid, u + 1)
                if not first:
                    act.wait_ge(dn_ps, g2 - 1)
                s.copy(hhi[:, k // 4 % 2, i], hid[:, k % 2]).then_inc(f_hi, 1)

            def expert_act(e, first=False):
                for k in range(8):
                    silu(8 * e + k, k)
                    if not (first and k == 0):
                        p = (k - 1) % 8
                        high(8 * e + (k - 1), p, 2 * e + (-1 if k == 0 else p // 4), p % 4, first)

            expert_act(0, first=True)
            with act.Fori(1, E) as e:
                expert_act(e, first=False)
            silu(8 * E, 0)
            high(8 * E - 1, 7, 2 * E - 1, 3, False)
            silu(8 * E + 1, 1)
            act.wait_ge(f_hid, 8 * E + 1)
            act.wait_ge(dn_ps, 2 * E - 1)
            s.copy(hhi[:, 0, 0], hid[:, 0]).then_inc(f_hi, 1)
            act.wait_ge(f_hid, 8 * E + 2)
            act.wait_ge(dn_ps, 2 * E)
            s.copy(hhi[:, 1, 0], hid[:, 1]).then_inc(f_hi, 1)
            root(8)

        @block.vector
        def _(dve):
            v = nc.vector
            n = [0]

            def settle(ins):
                n[0] += 1
                ins.then_inc(dve_step, 1)
                dve.wait_ge(dve_step, n[0])

            def inv_root(k, w, var, mul=1.0, add=EPS):
                v.tensor_scalar(rs[:, 0, 0:w], var, mul, add, ALU.mult, ALU.add).then_inc(sq_in, 1)
                dve.wait_ge(sq_in, k)
                dve.wait_ge(sq_out, k)
                settle(v.reciprocal(rs[:, 3, 0:w], rs[:, 1, 0:w]))
                settle(v.tensor_tensor(rs[:, 1, 0:w], rs[:, 3, 0:w], rs[:, 3, 0:w], ALU.mult))
                settle(v.tensor_tensor(rs[:, 1, 0:w], rs[:, 1, 0:w], rs[:, 0, 0:w], ALU.mult))
                settle(v.tensor_scalar(rs[:, 1, 0:w], rs[:, 1, 0:w], -0.5, 1.5, ALU.mult, ALU.add))
                settle(v.tensor_tensor(rs[:, 3, 0:w], rs[:, 3, 0:w], rs[:, 1, 0:w], ALU.mult))

            settle(v.memset(rs[:], 1.0))
            settle(v.memset(mv[:], 1.0))
            dve.wait_ge(ss_x, TC)
            inv_root(1, TC, ssx[:], 1.0 / D)
            for c in range(TC):
                last = v.tensor_scalar(xs2[:, c], x_sb[:, c].rearrange("p (q d) -> p q d", q=2).unsqueeze(2)
                                       .to_broadcast([P, 2, 2, HD]), rs[:, 3, c:c + 1], None, ALU.mult)
                last.then_inc(xs_ready, 1)
            dve.wait_ge(consts, 1)
            dve.wait_ge(xT_ps, 2 * TC)
            for q in range(2):
                v.tensor_copy(xT2[HD:P, q, 2:2 + T].rearrange("p (b n) -> p b n", b=2),
                              PS[HD:P, 2 * q:2 * q + 2, :]).then_inc(xT_v, 1)
            dve.wait_ge(w_ps, 1)
            for q in range(2):
                nw = V["nw_" + "fb"[q]]
                v.tensor_scalar(WcT[:, q, 0:2].rearrange("p g k c -> p (g k c)"), PS[:, 4 + 2 * q, :], nw, None, ALU.mult)
                v.tensor_scalar(WcT[:, q, 2].rearrange("p k c -> p (k c)"), PS[:, 5 + 2 * q, 0:2 * P], nw, None, ALU.mult)
                v.tensor_scalar(WzT[0:HD, q], PS[0:HD, 5 + 2 * q, 2 * P:3 * P], nw[0:HD], None, ALU.mult)
                v.tensor_scalar(WdT[0:HD, q], PS[0:HD, 5 + 2 * q, 3 * P:3 * P + 2], nw[0:HD], None,
                                ALU.mult).then_inc(w_sb, 1)
            dve.wait_ge(op_ps, 1)
            v.tensor_copy(opT, PS[:, 0, 0:P]).then_inc(op_sb, 1)
            dve.wait_ge(op_ps, 2)
            for q in range(2):
                v.tensor_scalar(Wout[:, q], PS[:, 1 + q, 0:P], V["gw_" + "fb"[q]], None,
                                ALU.mult).then_inc(op_sb, 1)
            dve.wait_ge(ld_aw, N_AW)
            for g, k in enumerate("ml"):
                settle(v.tensor_scalar(Tm[:, g], Epat[:], V["g_" + k], None, ALU.mult))
                v.tensor_copy(Tm[:, g, 0:1], V["b_" + k]).then_inc(t_ready, 1)
            for h in range(H):
                last = v.tensor_copy(VO[:, h, :, D:D + 1], I32[:, 0:1].unsqueeze(1).to_broadcast([P, 2, 1]))
            last.then_inc(t_ready, 1)

            dve.wait_ge(ld_ctx, N_CT)
            for c in range(CC):
                v.bn_stats(st6[:, c, :], ctx_sb[:, c, :])
            settle(v.bn_stats(st6[0:LEFT, CC, :], ctxl[:]))
            for c in range(CC):
                v.bn_aggr(mv[:, c, :], st6[:, c, :])
            settle(v.bn_aggr(mv[0:LEFT, CC, :], st6[0:LEFT, CC, :]))
            inv_root(2, CC + 1, mv[:, :, 1])
            settle(v.tensor_scalar(rs[:, 3], rs[:, 3], ZS, None, ALU.mult))
            v.scalar_tensor_tensor(out=rs[:, 2], in0=mv[:, :, 0], scalar=-1.0, in1=rs[:, 3], op0=ALU.mult,
                                   op1=ALU.mult).then_inc(zc_ready, 1)
            for i, (c0, w) in enumerate(KV_GROUPS + [(0, 1)]):
                dve.wait_ge(zt_ps, 2 * i + 2)
                k = w * P if c0 else LEFT
                v.tensor_copy(ZTlo[:, c0 * P:c0 * P + k], PS[:, 5 + 2 * (i % 2), 0:k]).then_inc(zt_lo, 1)

            dve.wait_ge(dt_ps, 1)
            bc = lambda t: t[:].unsqueeze(2).to_broadcast([P, 2, TC, 2])
            settle(v.tensor_tensor(dtc[:, 0], PS[:, 0, 0:4 * TC].rearrange("p (q c h) -> p q c h", q=2, c=TC), bc(dtb), ALU.add))
            fl = [dtc[:, i].rearrange("p q c h -> p (q c h)") for i in range(6)]
            v.scalar_tensor_tensor(out=fl[1], in0=fl[0], scalar=-1.0, in1=fl[0], op0=ALU.mult,
                                   op1=ALU.min).then_inc(dt_v, 1)
            dve.wait_ge(dt_a, 1)
            v.tensor_scalar(fl[2], fl[1], 1.0, None, ALU.add).then_inc(dt_v, 1)
            dve.wait_ge(dt_v, 2)
            dve.wait_ge(dt_a, 3)
            settle(v.tensor_scalar(fl[4], fl[2], -1.0, 1e-30, ALU.add, ALU.max))
            settle(v.reciprocal(fl[4], fl[4]))
            settle(v.tensor_tensor(fl[3], fl[3], fl[4], ALU.mult))
            settle(v.tensor_scalar(fl[4], fl[2], 1.0, None, ALU.is_equal))
            settle(v.tensor_tensor(fl[3], fl[3], fl[4], ALU.add))
            settle(v.tensor_tensor(fl[3], fl[3], fl[1], ALU.mult))
            v.scalar_tensor_tensor(out=fl[3], in0=fl[0], scalar=0.0, in1=fl[3], op0=ALU.max,
                                   op1=ALU.add).then_inc(dt_v, 1)
            v.tensor_scalar(Aneg[:], Aneg[:], -1.0, None, ALU.mult).then_inc(dt_v, 1)
            dve.wait_ge(dt_v, 4)
            v.tensor_tensor(dtc[:, 4], dtc[:, 3], bc(Aneg), ALU.mult).then_inc(dt_v, 1)

            def chunk_dve(c):
                for q in range(2):
                    b1 = PS[:, 4 * q + 1]
                    dve.wait_ge(t_done[q], c + 1)
                    after(dve, cdec_ready[q], c)
                    for h in range(2):
                        last = v.tensor_tensor_scan(Dec[:, q, h], b1[:, (2 + h) * P:(3 + h) * P], zer[:], 1.0,
                                                    ALU.mult, ALU.add)
                    last.then_inc(dec_ready[q], 1)
                    for h in range(2):
                        v.tensor_tensor_scan(LT[:, q, h], b1[:, (2 + h) * P:(3 + h) * P], I32[:], 0.0,
                                             ALU.mult, ALU.add)
                    after(dve, y_done[q], c)
                    after(dve, s_done[q], c)
                    v.tensor_tensor(xp_blocks(Xp, q), b1[:, 0:P].rearrange("p (h d) -> p h d", h=2),
                                    dtc[:, 3, q, c, :].unsqueeze(2).to_broadcast([P, 2, HD]), ALU.mult)
                    v.tensor_copy(Bm[:, q], b1[:, P:2 * P]).then_inc(b1_read[q], 1)
                    dve.wait_ge(b1_read[q], c + 1)
                    v.tensor_tensor(Xw[:, q].rearrange("p (h d) -> p h d", h=2), xp_blocks(Xp, q),
                                    LT[:, q, :, P - 1:P].to_broadcast([P, 2, HD]), ALU.mult).then_inc(xw_done[q], 1)
                    dve.wait_ge(g_done[q], c + 1)
                    v.tensor_tensor(Mt[:, q], LT[:, q], PS[:, 4 * q + 2, 0:P].unsqueeze(1).to_broadcast([P, 2, P]),
                                    ALU.mult).then_inc(m_done[q], 1)
                for q in range(2):
                    dve.wait_ge(y_done[q], c + 1)
                    v.scalar_tensor_tensor(out=y1[:, q], in0=xc[:, q], scalar=V["D_" + "fb"[q]],
                                           in1=PS[:, 4 * q + 3, 0:P], op0=ALU.mult, op1=ALU.add).then_inc(y1_done[q], 1)
                    dve.wait_ge(y1_done[q], c + 1)
                    after(dve, out_done[q], c)
                    after(dve, sq_done[q], c)
                    v.tensor_tensor(yg[:, q], y1[:, q], zs[:, q], ALU.mult).then_inc(yg_done[q], 1)
                    dve.wait_ge(s_done[q], c + 1)
                    v.tensor_tensor(Ht[:, q], xp_blocks(Hp, q), Dec[:, q, :, P - 1:P].to_broadcast([P, 2, HD]),
                                    ALU.mult).then_inc(ht_done[q], 1)
                    dve.wait_ge(ht_done[q], c + 1)
                    v.tensor_tensor(xp_blocks(Hp, q), Ht[:, q],
                                    PS[:, 4 * q + 2, P:2 * P].rearrange("p (h d) -> p h d", h=2),
                                    ALU.add).then_inc(h_done[q], 1)


            chunk_dve(0)
            with dve.Fori(1, TC) as c:
                chunk_dve(c)
            for q in range(2):
                dve.wait_ge(out_evac[q], TC)
            inv_root(3, 2 * TC, yo[:, :, :, D:D + 1].rearrange("p q c o -> p q (c o)"), 1.0 / D)
            rsv = rs[:, 3, 0:2 * TC].rearrange("p (q c) -> p q c", q=2)
            for q in (1, 0):
                v.tensor_tensor(yo[:, q, :, 0:D], yo[:, q, :, 0:D],
                                rsv[:, q].unsqueeze(2).to_broadcast([P, TC, D]), ALU.mult).then_inc(yo_ready, 1)
            dve.wait_ge(yo_ready, 2)
            settle(v.scalar_tensor_tensor(out=x_sb, in0=x_sb, scalar=2.0, in1=yo[:, 0, :, 0:D], op0=ALU.mult, op1=ALU.add))
            settle(v.tensor_tensor(x_sb, x_sb, opb[:].unsqueeze(1).to_broadcast([P, TC, D]), ALU.add))
            dve.wait_ge(J_ps, 2)
            settle(v.tensor_tensor(x_sb.rearrange("p c d -> p (c d)").rearrange("p (b n) -> p b n", b=2),
                                   x_sb.rearrange("p c d -> p (c d)").rearrange("p (b n) -> p b n", b=2),
                                   PS[:, 0:2, :], ALU.add))

            def norm_stats(t, k):
                for c in range(TC):
                    last = v.bn_stats(st6[:, c, :], t[:, c, :])
                settle(last)
                for c in range(TC):
                    last = v.bn_aggr(mv[:, c, :], st6[:, c, :])
                settle(last)
                inv_root(k, TC, mv[:, 0:TC, 1])

            def norm_rows(dst, src):
                for c in range(TC):
                    last = v.tensor_scalar(dst[:, c, :], src[:, c, :], mv[:, c, 0:1], rs[:, 3, c:c + 1],
                                           ALU.subtract, ALU.mult)
                return last

            norm_stats(x_sb, 4)
            settle(norm_rows(x_sb, x_sb))
            v.tensor_tensor(acc[:], x_sb, boB[:].unsqueeze(1).to_broadcast([P, TC, D]), ALU.add)
            norm_stats(x_sb, 5)
            settle(v.tensor_scalar(rs[:, 3, 0:TC], rs[:, 3, 0:TC], ZS, None, ALU.mult))
            norm_rows(x_sb, x_sb).then_inc(zl_ready, 1)
            for i in range(2):
                dve.wait_ge(zlT_a, 2 * i + 2)
                at = slice(LAT0 * P + i * QB, LAT0 * P + (i + 1) * QB)
                v.tensor_tensor(ZTlo[:, at], PS[:, i, :], ZThi[:, at], ALU.subtract).then_inc(zlT_v, 1)

            def a_head(b):
                if not (isinstance(b, int) and b == 0):
                    dve.wait_ge(a_ps, 2 * b)
                v.tensor_copy(A_now[:], AH[:, b % H]).then_inc(a_stage, 1)

            def a_low(b):
                for g in range(2):
                    dve.wait_ge(a_hi, 2 * b + g + 1)
                    v.tensor_copy(R0[0:1, g, :], PS[0:1, 7 - g, :]).then_inc(r0_done, 1)
                    v.tensor_tensor(A[:, b % 4, 2 * g + 1, :], PS[:, 7 - g, :], A[:, b % 4, 2 * g, :],
                                    ALU.subtract).then_inc(a_lo, 1)

            def unit_max(n, par, kb, i):
                dve.wait_ge(mx_done, n + 1)
                w = 2 * P + LEFT if isinstance(kb, int) and kb == KB_LEFT else QB
                v.tensor_reduce(mxs[:, i, bass.ds(kb, 1)], PS[:, 6 + par, 0:w], AX.X, ALU.max).then_inc(mx_read, 1)

            def max_column(b):
                dve.wait_ge(mx_read, NU * b + NU)
                v.tensor_reduce(mcol[:, 0, :], mxs[:], AX.X, ALU.max).then_inc(m_col, 1)
                dve.wait_ge(m_col, b + 1)
                v.tensor_scalar(mcol[:, 1, :], mcol[:, 0, :], -1.0 / ZS, LIFT * AS, ALU.mult, ALU.add).then_inc(m_neg, 1)

            def max_row(b):
                dve.wait_ge(m_row, b + 1)
                dve.wait_ge(r0_done, 2 * b + 2)
                v.tensor_tensor(R0[:], R0[:], PS[0:1, 6, :].unsqueeze(1).to_broadcast([1, 2, QB]),
                                ALU.add).then_inc(row_sum, 1)
                pair = A[0:1, b % 4].rearrange("p (g k) n -> p g k n", g=2)
                dve.wait_ge(row_sum, b + 1)
                v.tensor_copy(pair[:, :, 0, :], R0[:]).then_inc(row_hi, 1)
                dve.wait_ge(row_hi, b + 1)
                v.tensor_tensor(pair[:, :, 1, :], R0[:], pair[:, :, 0, :], ALU.subtract).then_inc(row_lo, 1)

            def low(j, st):
                g, (r, _) = step_number(j, st), place_of(st)
                w = len(STEPS[r]) * QB
                dve.wait_ge(p32_ready, g + 1)
                v.tensor_tensor(Plo[:, r % 3, 0:w], P32[:, r % 2, 0:w], Phi[:, r % 3, 0:w],
                                ALU.subtract).then_inc(lo_ready, 1)

            def project_acc(b, k):
                o = PS[:, 7 - k].rearrange("p (i n) -> p i n", n=256)
                dve.wait_ge(o_ps, 2 * b + k + 1)
                v.reciprocal(rden[:, 2 * k:2 * k + 2].unsqueeze(2), o[:, :, D:D + 1]).then_inc(o_rd, 1)
                dve.wait_ge(o_rd, 2 * b + k + 1)
                for i in range(2):
                    t = b // H * 4 + 2 * k + i
                    last = v.scalar_tensor_tensor(out=acc[:, t, :], in0=o[:, i, 0:D], scalar=rden[:, 2 * k + i:2 * k + i + 1],
                                                  in1=acc[:, t, :], op0=ALU.mult, op1=ALU.add)
                last.then_inc(o_acc, 1)

            def block_dve(j, first=False, maxes=True, nxt=True):
                b, u = j + 1, 0
                for st in range(LOOP0):
                    if maxes:
                        for _ in range(UNITS_HEAD[st]):
                            unit_max(NU * b + u, u % 2, KB_LEFT + u // 4, u % 4)
                            u += 1
                    low(j, st)
                with dve.Fori(0, LOOPN) as i:
                    u = 0
                    for k in range(6):
                        if maxes:
                            for _ in range(UNITS_TURN[k]):
                                unit_max(NU * b + 16 * i + (12 + u), u % 2, 4 * i + u // 4, u % 4)
                                u += 1
                        low(j, Turn(i, k))
                if maxes:
                    max_column(b)
                for st in range(TAIL, NS):
                    low(j, st)
                    if st == TAIL and maxes:
                        max_row(b)
                        if nxt:
                            a_head(j + 2)
                    if st in (TAIL + 1, TAIL + 2) and not first:
                        project_acc(j - 1, st - TAIL - 1)
                    if st == NS - 2 and nxt:
                        a_low(j + 2)

            a_head(0)
            a_low(0)
            with dve.Fori(0, KB_LEFT) as kb:
                for i in range(4):
                    unit_max(4 * kb + i, i % 2, kb, i)
            for u in range(4 * KB_LEFT, NU):
                unit_max(u, u % 2, u // 4, u % 4)
            max_column(0)
            max_row(0)
            a_head(1)
            a_low(1)
            block_dve(0, first=True)
            with dve.Fori(1, NBLK - 2) as j:
                block_dve(j)
            block_dve(NBLK - 2, nxt=False)
            block_dve(NBLK - 1, maxes=False, nxt=False)
            project_acc(NBLK - 1, 0)
            project_acc(NBLK - 1, 1)

            dve.wait_ge(o_acc, 2 * NBLK)
            norm_stats(acc, 6)
            settle(norm_rows(acc, acc))
            norm_stats(acc, 7)
            norm_rows(xf, acc).then_inc(xf_ready, 1)
            dve.wait_ge(ld_fv, N_FV)
            for i in range(2):
                dve.wait_ge(xfT_ps, 4 * i + 4)
                v.tensor_scalar(xfT[:, i * QB:(i + 1) * QB], PS[:, i, :], V["g_f"], V["b_f"], ALU.mult,
                                ALU.add).then_inc(xfT_v, 1)
            dve.wait_ge(xf_hi, 1)
            v.scalar_tensor_tensor(out=xflo, in0=xfT, scalar=XS, in1=xfhi, op0=ALU.mult, op1=ALU.subtract).then_inc(xf_lo, 1)
            dve.wait_ge(rt_ps, 1)
            settle(v.tensor_copy(lg[:], PS[:, 2, 0:TC * E].rearrange("p (c e) -> p c e", c=TC)))
            settle(v.tensor_reduce(rt[:, 0, :].unsqueeze(2), lg[:], AX.X, ALU.max))
            v.tensor_scalar(rt[:, 0, :], rt[:, 0, :], -1.0, None, ALU.mult).then_inc(rt_v, 1)
            dve.wait_ge(rt_a, TC)
            settle(v.reciprocal(rt[:, 1, :], rt[:, 1, :]))
            settle(v.tensor_tensor(pr[:], pr[:], rt[:, 1, :].unsqueeze(2).to_broadcast([P, TC, E]), ALU.mult))
            for c in range(TC):
                last = v.max(mx8[:, c], pr[:, c])
            settle(last)
            for c in range(TC):
                last = v.max_index(ix8[:, c], mx8[:, c], pr[:, c])
            settle(last)
            settle(v.tensor_copy(ixf[:], ix8[:]))
            settle(v.tensor_tensor(rt[:, 2, :].unsqueeze(2), mx8[:, :, 0:1], mx8[:, :, 1:2], ALU.add))
            settle(v.reciprocal(rt[:, 2, :], rt[:, 2, :]))
            settle(v.tensor_scalar(rt[:, 2, :], rt[:, 2, :], 1 / (HS * WS), None, ALU.mult))
            settle(v.tensor_tensor(mx8[:, :, 0:2], mx8[:, :, 0:2],
                                   rt[:, 2, :].unsqueeze(2).to_broadcast([P, TC, 2]), ALU.mult))
            for k, dst in ((0, cb), (1, cb2)):
                settle(v.tensor_tensor(dst[:], iota8[:].unsqueeze(1).to_broadcast([P, TC, E]),
                                       ixf[:, :, k:k + 1].to_broadcast([P, TC, E]), ALU.is_equal))
                settle(v.tensor_tensor(dst[:], dst[:], mx8[:, :, k:k + 1].to_broadcast([P, TC, E]), ALU.mult))
            settle(v.tensor_tensor(cb[:], cb[:], cb2[:], ALU.add))

            def clip(u, k):
                dve.wait_ge(f_ps, u + 1)
                if not (isinstance(u, int) and u < 2):
                    dve.wait_ge(f_silu, u - 1)
                lim = 10.0 * XS * WS
                v.tensor_scalar(gcl[:, k % 2], PS[:, 2 * (k % 2)], lim, -lim, ALU.min, ALU.max).then_inc(f_clip, 1)

            def hidden(u, k):
                dve.wait_ge(f_silu, u + 1)
                if not (isinstance(u, int) and u < 2):
                    dve.wait_ge(f_hi, u - 1)
                    dve.wait_ge(f_lo, u - 1)
                v.scalar_tensor_tensor(out=hid[:, k % 2], in0=PS[:, 2 * (k % 2) + 1], scalar=HS / (XS * WS),
                                       in1=sil[:, k % 2], op0=ALU.mult, op1=ALU.mult).then_inc(f_hid, 1)

            def hidden_low(u, k, half, i):
                dve.wait_ge(f_hi, u + 1)
                v.tensor_tensor(hlo[:, half, i], hid[:, k % 2], hhi[:, half, i], ALU.subtract).then_inc(f_lo, 1)

            def down_acc(g2, e, half):
                dve.wait_ge(dn_ps, g2 + 1)
                if not (isinstance(g2, int) and g2 == 0):
                    dve.wait_ge(dn_acc, g2)
                for t in range(4):
                    c = half * 4 + t
                    share = 1 / (HS * WS) if isinstance(e, int) and e == E else cb[:, c, bass.ds(e, 1)]
                    last = v.scalar_tensor_tensor(out=acc[:, c, :], in0=PS[:, 6 + half, t * P:(t + 1) * P], scalar=share,
                                                  in1=acc[:, c, :], op0=ALU.mult, op1=ALU.add)
                last.then_inc(dn_acc, 1)

            def expert_dve(e, first=False):
                for k in range(8):
                    u = 8 * e + k
                    clip(u, k)
                    if not (first and k < 1):
                        hidden(u - 1, (k - 1) % 8)
                    if not (first and k < 2):
                        m = (k - 2) % 8
                        hidden_low(u - 2, m, m // 4, m % 4)
                    if k == 3 and not first:
                        down_acc(2 * e - 1, e - 1, 1)
                    if k == 7:
                        down_acc(2 * e, e, 0)

            expert_dve(0, first=True)
            with dve.Fori(1, E) as e:
                expert_dve(e)
            last_u = 8 * E
            clip(last_u, 0)
            hidden(last_u - 1, 7)
            hidden_low(last_u - 2, 6, 1, 2)
            clip(last_u + 1, 1)
            hidden(last_u, 0)
            hidden_low(last_u - 1, 7, 1, 3)
            hidden(last_u + 1, 1)
            hidden_low(last_u, 0, 0, 0)
            down_acc(2 * E - 1, E - 1, 1)
            hidden_low(last_u + 1, 1, 1, 0)
            down_acc(2 * E, E, 0)
            down_acc(2 * E + 1, E, 1)
            dve.wait_ge(dn_acc, 2 * E + 2)
            norm_stats(acc, 8)
            for c in range(TC):
                v.tensor_scalar(xf[:, c, :], acc[:, c, :], mv[:, c, 0:1], rs[:, 3, c:c + 1],
                                ALU.subtract, ALU.mult).then_inc(fin, 1)

        @block.tensor
        def _(pe):
            t = nc.tensor

            def mm(o, l, r, start=True, stop=True):
                return t.matmul(o, l, r, start=start, stop=stop)

            pe.wait_ge(consts, 1)
            for c in range(TC):
                pe.wait_ge(xs_ready, c + 1)
                for q in range(2):
                    at = c if q == 0 else TC - 1 - c
                    mm(PS[:, 2 * q + at // 4, at % 4 * P:(at % 4 + 1) * P], xs2[:, c, q].rearrange("p k d -> p (k d)"),
                       (I32, J32)[q][:]).then_inc(xT_ps, 1)
            pe.wait_ge(iwk_ready, 1)
            for q in range(2):
                for r in range(3):
                    for k in range(2):
                        o = (2 * r + k) * P
                        t.transpose(PS[:, 4 + 2 * q + o // 512, o % 512:o % 512 + P],
                                    iwk[:, q, r, 2 * k:2 * k + 2].rearrange("p k d -> p (k d)"), I32[:])
                t.transpose(PS[0:HD, 5 + 2 * q, 2 * P:3 * P], iw[:, q, 0], I32[:])
                last = t.transpose(PS[0:HD, 5 + 2 * q, 3 * P:3 * P + 2], iwdt[0:2, q], I32[0:2, 0:2])
            last.then_inc(w_ps, 1)
            pe.wait_ge(xT_a, 2)
            pe.wait_ge(xT_v, 2)
            t.transpose(PS[:, 0, 0:P], opw, I32[:]).then_inc(op_ps, 1)
            pe.wait_ge(op_sb, 1)
            for q in range(2):
                r = slice(HD * q, HD * q + HD)
                last = mm(PS[:, 1 + q, 0:P], ow[r, :], opT[r, :])
            last.then_inc(op_ps, 1)
            pe.wait_ge(w_sb, 2)
            for q in range(2):
                for c in range(TC):
                    o = 2 * (q * TC + c)
                    last = mm(PS[:, 0, o:o + 2], xT2[0:HD, q, 3 + c * P:3 + (c + 1) * P], WdT[0:HD, q])
            last.then_inc(dt_ps, 1)

            for i, (c0, w) in enumerate(KV_GROUPS + [(0, 1)]):
                for src, s_rdy, s_free, o in ((Zhi, z_hi, zt_hi, 0), (Zlo, z_lo, zt_lo, 1)):
                    pe.wait_ge(s_rdy, i + 1)
                    if i >= 2:
                        pe.wait_ge(s_free, i - 1)
                    for k in range(w):
                        n = P if c0 else LEFT
                        last = mm(PS[:, 4 + 2 * (i % 2) + o, k * P:k * P + n], src[0:n, c0 + k, :], I16[0:n, 0:n])
                    last.then_inc(zt_ps, 1)
            pe.wait_ge(zt_hi, len(KV_GROUPS) + 1)
            pe.wait_ge(zt_lo, len(KV_GROUPS) + 1)

            pe.wait_ge(op_sb, 3)
            pe.wait_ge(dt_v, 1)
            def chunk_pe(c):
                for q in range(2):
                    b0 = PS[:, 4 * q]
                    after(pe, silu_done[q], 4 * c)
                    mm(b0[:, 0:P], WzT[0:HD, q], xT2[0:HD, q, bass.ds(c * P + 3, P)])
                    for r in range(3):
                        for k in range(2):
                            last = mm(b0[:, (r + 1) * P:(r + 2) * P], WcT[:, q, r, k],
                                      xT2[:, q, bass.ds(c * P + 2 * k, P)], start=k == 0, stop=k == 1)
                    last.then_inc(conv_done[q], 1)
                for q in range(2):
                    b1 = PS[:, 4 * q + 1]
                    after(pe, b1_read[q], c)
                    pe.wait_ge(dg_ready[q], c + 1)
                    mm(b1[:, 2 * P:4 * P], ones[:], dg[:, q].rearrange("p h n -> p (h n)"))
                    pe.wait_ge(silu_done[q], 4 * c + 4)
                    t.transpose(b1[:, 0:P], xc[:, q], I32[:])
                    t.transpose(b1[:, P:2 * P], Bc[:, q], I32[:]).then_inc(t_done[q], 1)
                    after(pe, h_done[q], c)
                    mm(PS[:, 4 * q + 2, 0:P], Bc[:, q], Cc[:, q]).then_inc(g_done[q], 1)
                for q in range(2):
                    pe.wait_ge(m_done[q], c + 1)
                    pe.wait_ge(xw_done[q], c + 1)
                    mm(PS[:, 4 * q + 2, P:2 * P], Bm[:, q], Xw[:, q]).then_inc(s_done[q], 1)
                    pe.wait_ge(cdec_ready[q], c + 1)
                    after(pe, out_evac[q], c)
                    for k, (l, r) in enumerate(((Xp, Mt), (Hp, CD))):
                        for h in range(2):
                            last = mm(PS[:, 4 * q + 3, 0:P], l[:, q, h * P:(h + 1) * P], r[:, q, h],
                                      start=k + h == 0, stop=k + h == 2)
                    last.then_inc(y_done[q], 1)
                for q in range(2):
                    pe.wait_ge(yg_done[q], c + 1)
                    mm(PS[:, 4 * q + 3, P:2 * P], yg[:, q], Wout[:, q])
                    pe.wait_ge(sq_done[q], c + 1)
                    mm(PS[:, 4 * q + 3, 2 * P:2 * P + 1], sq[:, q], ones[:, 0:1]).then_inc(out_done[q], 1)

            chunk_pe(0)
            with pe.Fori(1, TC) as c:
                chunk_pe(c)
            pe.wait_ge(yo_ready, 1)
            for i in range(2):
                mm(PS[:, i, :], J32[:], yo[:, 1, 4 * i:4 * i + 4, 0:D]).then_inc(J_ps, 1)

            pe.wait_ge(out_evac[0], TC)
            pe.wait_ge(h_done[0], TC)
            pe.wait_ge(t_ready, 3)
            pe.wait_ge(bsel_ready, 1)
            pe.wait_ge(ld_b, 32)
            for h in range(H):
                hs = slice(h * D, (h + 1) * D)
                if h:
                    pe.wait_ge(wt_sb, 2 * h)
                b2, b3 = PS[:, 2], PS[:, 3]
                both = Tm[:].rearrange("p g d -> p (g d)")
                mm(b2[:, 0:P], Wq[:, hs], Tm[:, 1], stop=False)
                mm(b2[:, 0:P], brow[0:3, hs], bsel[0:3, 0, 0], start=False)
                mm(b2[:, P:3 * P], Wkv[:, hs], both, stop=False)
                mm(b2[:, P:3 * P], brow[0:3, hs], bsel[0:3, 1].rearrange("p g n -> p (g n)"), start=False).then_inc(wt_ps, 1)
                mm(b3[:, 0:2 * P], Wkv[:, H * D + h * D:H * D + (h + 1) * D], both, stop=False)
                mm(b3[:, 0:2 * P], brow[0:3, hs], bsel[0:3, 2].rearrange("p g n -> p (g n)"), start=False).then_inc(wt_ps, 1)
                pe.wait_ge(wt_sb, 2 * h + 2)
                if h:
                    pe.wait_ge(ah_sb, 2 * h)
                mm(PS[:, 4, 0:2 * P], WT[:, 0:P], WT[:, P:3 * P])
                for g in range(2):
                    last = mm(PS[:, 5, g * P:(g + 1) * P], WT[:, (3 + g) * P:(4 + g) * P], Wo[:, h])
                last.then_inc(ah_ps, 1)

            pe.wait_ge(z_hi, len(KV_GROUPS) + 2)
            for c in range(TC):
                t.transpose(PS[:, c // 4, c % 4 * P:(c % 4 + 1) * P], x_sb[:, c, :], I32[:]).then_inc(zlT_ps, 1)

            def a_side(b):
                pe.wait_ge(a_stage, b + 1)
                tokens = bass.ds((b // H) * QB, QB)
                for g in range(2):
                    mm(PS[:, 7 - g, :], A_now[:, g], zlT[:, tokens]).then_inc(a_ps, 1)

            def scores(j, st, ring, i):
                g, (r, turn) = step_number(j, st), place_of(st)
                if i >= len(STEPS[r]):
                    return
                if i == 0:
                    if not early(j, st, 2):
                        pe.wait_ge(p32_ready, g - 1)
                    if r == 0:
                        pe.wait_ge(row_lo, j + 1)
                ch = STEPS[r][i]
                o = PS[:, 2 * (r % 2) + i, :]
                k = 2 if is_latent(ch) else 0
                zh, zl = (z[:, bass.ds(turn * (12 * P) + ch * P, P)] for z in (ZThi, ZTlo))
                mm(o, zh, A[:, ring, k, :], stop=False)
                mm(o, zh, A[:, ring, k + 1, :], start=False, stop=False)
                last = mm(o, zl, A[:, ring, k, :], start=False)
                if i == len(STEPS[r]) - 1:
                    last.then_inc(qk_done, 1)

            def sums(r, turn, i):
                ch = STEPS[r][i]
                latent = is_latent(ch)
                return (PS[:, 5 if latent else 4, :], ch == (LAT0 if latent else 0),
                        ch == (CTX0 - 1 if latent else NCH - 1), Zhi[:, turn * 12 + ch, :], Zlo[:, turn * 12 + ch, :])

            def values_high(g, r, turn=0):
                pe.wait_ge(hi_ready, g + 1)
                for i in range(len(STEPS[r])):
                    o, first, _, zh, zl = sums(r, turn, i)
                    p = Phi[:, r % 3, i * QB:(i + 1) * QB]
                    mm(o, zh, p, start=first, stop=False)
                    mm(o, zl, p, start=False, stop=False)

            def values_low(g, r, turn=0):
                pe.wait_ge(lo_ready, g + 1)
                for i in range(len(STEPS[r])):
                    o, _, end, zh, _ = sums(r, turn, i)
                    last = mm(o, zh, Plo[:, r % 3, i * QB:(i + 1) * QB], start=False, stop=end)
                last.then_inc(pv_done, 1)

            def unit(n, par, kb, i, ring):
                if not (isinstance(n, int) and n < 2):
                    pe.wait_ge(mx_read, n - 1)
                static = isinstance(kb, int)
                latent = static and kb >= KB_LAT
                w = 2 * P if static and kb == KB_LEFT else QB
                at = LAT0 * P + (kb - KB_LAT) * QB if latent else kb * QB + CTX0 * P
                q = A[:, ring, 2 if latent else 0, i * P:(i + 1) * P]
                last = mm(PS[:, 6 + par, 0:w], q, ZThi[:, bass.ds(at, w)])
                if w < QB:
                    last = mm(PS[:, 6 + par, w:w + LEFT], q, ZThi[:, 0:LEFT])
                last.then_inc(mx_done, 1)

            def max_to_row(b):
                pe.wait_ge(m_neg, b + 1)
                for i in range(4):
                    last = mm(PS[0:1, 6, i * P:(i + 1) * P], mcol[:, 1, i:i + 1], I32[:])
                last.then_inc(m_row, 1)

            def project(b, k):
                pe.wait_ge(u_evac, b + 1)
                for i in range(2):
                    for g in range(2):
                        at = (2 * k + i) * P
                        last = mm(PS[:, 7 - k, 256 * i:256 * i + D + 2], U_sb[:, g, at:at + P], VO[:, b % H, g, :],
                                  start=g == 0, stop=g == 1)
                last.then_inc(o_ps, 1)

            def slots(units):
                return (units[0:1], units[1:2], units[2:3]) if len(units) == 3 else (units[0:1], [], units[1:2])

            def block_pe(j, first=False, maxes=True, nxt=True):
                b = j + 1
                ring, nring = j % 4, (j + 1) % 4
                u = 0
                for st in range(LOOP0):
                    units = list(range(u, u + UNITS_HEAD[st])) if maxes else []
                    u += UNITS_HEAD[st]
                    s0, s1, s2 = slots(units)
                    lag = st - 2 if st >= 2 else NS + st - 2
                    lagged = NS * j + st - 2 if st >= 2 or not first else None

                    def some(us):
                        for w in us:
                            unit(NU * b + w, w % 2, KB_LEFT + w // 4, w % 4, nring)

                    scores(j, st, ring, 0)
                    if st == 1 and maxes:
                        pe.wait_ge(a_lo, 2 * b + 2)
                    some(s0)
                    scores(j, st, ring, 1)
                    some(s1)
                    if lagged is not None:
                        if st == 2 and not first:
                            pe.wait_ge(u_evac, j)
                        values_high(lagged, lag)
                    some(s2)
                    if lagged is not None:
                        values_low(lagged, lag)
                with pe.Fori(0, LOOPN) as i:
                    u = 0
                    for k in range(6):
                        units = list(range(u, u + UNITS_TURN[k])) if maxes else []
                        u += UNITS_TURN[k]
                        s0, s1, s2 = slots(units)
                        lagged, lag = NS * j + 6 * i + (LOOP0 + k - 2), LOOP0 + k - 2

                        def some(us):
                            for w in us:
                                unit(NU * b + 16 * i + (12 + w), w % 2, 4 * i + w // 4, w % 4, nring)

                        scores(j, Turn(i, k), ring, 0)
                        some(s0)
                        scores(j, Turn(i, k), ring, 1)
                        some(s1)
                        values_high(lagged, lag, i)
                        some(s2)
                        values_low(lagged, lag, i)
                for st in range(TAIL, NS):
                    scores(j, st, ring, 0)
                    scores(j, st, ring, 1)
                    if st == TAIL + 1 and maxes:
                        max_to_row(b)
                    if st == TAIL + 2 and not first:
                        project(j - 1, 0)
                    if st == TAIL + 3:
                        if maxes:
                            pe.wait_ge(row_sum, b + 1)
                        if not first:
                            project(j - 1, 1)
                        if nxt:
                            if not first:
                                pe.wait_ge(o_acc, 2 * j)
                            a_side(j + 2)
                    values_high(NS * j + (st - 2), st - 2)
                    values_low(NS * j + (st - 2), st - 2)

            pe.wait_ge(zlT_a, 4)
            pe.wait_ge(zlT_v, 2)
            pe.wait_ge(z_lo, len(KV_GROUPS) + 2)
            pe.wait_ge(ah_sb, 2 * H)
            a_side(0)
            pe.wait_ge(a_lo, 2)
            def four_units(kb):
                for i in range(4):
                    unit(4 * kb + i, i % 2, kb, i, 0)

            four_units(0)
            with pe.Fori(1, KB_LEFT) as kb:
                four_units(kb)
            for u in range(4 * KB_LEFT, NU):
                unit(u, u % 2, u // 4, u % 4, 0)
            max_to_row(0)
            pe.wait_ge(row_sum, 1)
            a_side(1)
            block_pe(0, first=True)
            with pe.Fori(1, NBLK - 2) as j:
                block_pe(j)
            block_pe(NBLK - 2, nxt=False)
            block_pe(NBLK - 1, maxes=False, nxt=False)
            for r in (NS - 2, NS - 1):
                values_high(NS * (NBLK - 1) + r, r)
                values_low(NS * (NBLK - 1) + r, r)
            pe.wait_ge(o_acc, 2 * (NBLK - 1))
            project(NBLK - 1, 0)
            project(NBLK - 1, 1)

            pe.wait_ge(xf_ready, 1)
            for c in range(TC):
                t.transpose(PS[:, c // 4, c % 4 * P:(c % 4 + 1) * P], xf[:, c, :], I32[:]).then_inc(xfT_ps, 1)
            pe.wait_ge(xfT_v, 2)
            for c in range(TC):
                last = mm(PS[:, 2, c * E:(c + 1) * E], xfT[:, c * P:(c + 1) * P], rw[:])
            last.then_inc(rt_ps, 1)
            pe.wait_ge(xf_hi, 1)
            pe.wait_ge(xf_lo, 1)
            pe.wait_ge(rt_v, 1)

            def gate_up(u, k, hi, lo, f0, half):
                if not (isinstance(u, int) and u < 2):
                    pe.wait_ge(f_hid, u - 1)
                xh, xl = (x[:, half * QB:(half + 1) * QB] for x in (xfhi, xflo))
                for o, at in enumerate(f0):
                    bank, c = PS[:, 2 * (k % 2) + o], slice(at, at + P)
                    mm(bank, hi[:, c], xh, stop=False)
                    mm(bank, hi[:, c], xl, start=False, stop=False)
                    last = mm(bank, lo[:, c], xh, start=False)
                last.then_inc(f_ps, 1)

            def down(g2, n_low, half, his, los):
                pe.wait_ge(f_lo, n_low)
                if not (isinstance(g2, int) and g2 < 2):
                    pe.wait_ge(dn_acc, g2 - 1)
                n = len(his)
                for c in range(4):
                    for i in range(n):
                        hh, hl = (h[:, half, i, c * P:(c + 1) * P] for h in (hhi, hlo))
                        o = PS[:, 6 + half, c * P:(c + 1) * P]
                        mm(o, hh, his[i], start=i == 0, stop=False)
                        mm(o, hh, los[i], start=False, stop=False)
                        last = mm(o, hl, his[i], start=False, stop=i == n - 1)
                last.then_inc(dn_ps, 1)

            def routed_down(g2, e, half, n_low):
                down(g2, n_low, half, [DNhi[:, e, i, :] for i in range(4)], [DNlo[:, e, i, :] for i in range(4)])

            def expert_pe(e, first=False):
                pe.wait_ge(stage_used, NPART * e + NPART)
                for k in range(8):
                    gate_up(8 * e + k, k, GUhi[:, e], GUlo[:, e], (k % 4 * P, F + k % 4 * P), k // 4)
                    if k == 2 and not first:
                        routed_down(2 * e - 1, e - 1, 1, 8 * e)
                    if k == 6:
                        routed_down(2 * e, e, 0, 8 * e + 4)

            expert_pe(0, first=True)
            with pe.Fori(1, E) as e:
                expert_pe(e)
            pe.wait_ge(stage_used, NPART * E + 2)
            for half in range(2):
                gate_up(8 * E + half, half, SGhi, SGlo, (0, FS), half)
            routed_down(2 * E - 1, E - 1, 1, 8 * E)
            for half in range(2):
                down(2 * E + half, 8 * E + half + 1, half, [SDhi], [SDlo])


_NAMES = {
    "x": "x", "ctx_1024": "ctx", "L0_attn_norm_w": "norm_w", "L0_attn_op_w": "op_w", "L0_attn_op_b": "op_b",
    "L0_xattn_gamma_media": "gamma_media", "L0_xattn_beta_media": "beta_media", "L0_xattn_gamma_lat": "gamma_lat",
    "L0_xattn_beta_lat": "beta_lat", "L0_xattn_Wq": "Wq", "L0_xattn_bq": "bq", "L0_xattn_Wkv": "Wkv",
    "L0_xattn_bkv": "bkv", "L0_xattn_Wo": "Wo", "L0_xattn_bo": "bo", "L0_ffn_ln_gamma": "ln_gamma",
    "L0_ffn_ln_beta": "ln_beta", "L0_ffn_router_w": "router_w", "L0_ffn_gate_up_w": "gate_up_w",
    "L0_ffn_down_w": "down_w", "L0_ffn_shared_gate_up_w": "shared_gate_up_w", "L0_ffn_shared_down_w": "shared_down_w",
}
_MAMBA = ["in_w", "conv_w", "conv_b", "dt_bias", "A_log", "D", "gnorm_w", "outp_w"]


def kernel(**inputs):
    import numpy as _np
    import concourse.bacc as _bacc
    from concourse.bass_utils import run_bass_kernel_spmd as _run

    nc = _bacc.Bacc("TRN2", target_bir_lowering=False, num_devices=1)
    arrays = {}

    def dram(name):
        x = _np.ascontiguousarray(inputs[name])
        arrays[f"in_{name}"] = x
        return nc.dram_tensor(f"in_{name}", x.shape, mybir.dt.from_np(x.dtype), kind="ExternalInput").ap()

    a = {short: dram(name) for name, short in _NAMES.items()}
    for q in "fb":
        a[q] = {m: dram(f"L0_attn_{q}_{m}") for m in _MAMBA}
    out = nc.dram_tensor("out_0", (1, T, D), F32, kind="ExternalOutput").ap()
    layer(nc, a, out)
    return _run(nc, [arrays], core_ids=[0]).results[0]["out_0"]
```

```python
import numpy as np
from contextlib import ExitStack

import concourse.bass as bass
from concourse import mybir

F32, F16, U32 = mybir.dt.float32, mybir.dt.float16, mybir.dt.uint32
ACT, ALU, AX = mybir.ActivationFunctionType, mybir.AluOpType, mybir.AxisListType

P = 128
D = 128
T = 1024
TC = T // P
CTX = 6404
CC = CTX // P
LEFT = CTX - CC * P
HD = 64
H = 8
E, F, FS = 8, 512, 128
EPS = 1e-5
NCH = 1 + TC + CC
LAT0, CTX0 = 1, 1 + TC
QB = 512
NBLK = H * T // QB
ZS, AS, AHS = 16.0, 64.0, 16.0
SSC = ZS * AS
LIFT = 8 * float(np.log(2))
XS, WS, HS = 16.0, 64.0, 4.0

STEPS = [[0, 1], [2, 3], [4, 5], [6, 7], [8]] + [[CTX0 + 2 * i, CTX0 + 2 * i + 1] for i in range(CC // 2)]
NS = len(STEPS)
assert NS % 6 == 0
LOOP0, LOOPN = 7, 3
TAIL = LOOP0 + 6 * LOOPN
KB = 15
KB_LEFT, KB_LAT = 12, 13
NU = KB * 4
UNITS_HEAD = [0, 2, 2, 2, 2, 2, 2]
UNITS_TURN = [3, 3, 3, 3, 2, 2]
RING = 4
NPART = 6


TILES = [([2], [3]), ([], []), ([], [4]), ([], [5]), ([6], [7]), ([], []), ([], [0]), ([], [1])]


def is_latent(chunk):
    return LAT0 <= chunk < CTX0


class Turn:

    def __init__(self, i, k):
        self.i, self.k = i, k


def step_number(j, st):
    return NS * j + 6 * st.i + (LOOP0 + st.k) if isinstance(st, Turn) else NS * j + st


def place_of(st):
    return (LOOP0 + st.k, st.i) if isinstance(st, Turn) else (st, 0)


def early(j, st, n):
    return isinstance(j, int) and j == 0 and isinstance(st, int) and st < n


def after(eng, s, n):
    if not (isinstance(n, int) and n == 0):
        eng.wait_ge(s, n)


def layer(nc, a, out):
    ctx = ExitStack()
    with ctx:
        def sb(name, shape, dt=F32):
            return ctx.enter_context(nc.sbuf_tensor(name, shape, dt))

        sems = {}

        def sem(name):
            sems[name] = ctx.enter_context(nc.semaphore(name))
            return sems[name]

        def carve(arena):
            at = [0]

            def take(shape, dt=F32, p=P):
                n = int(np.prod(shape))
                words = n if dt != F16 else (n + 1) // 2
                v = arena[0:p, at[0]:at[0] + words]
                at[0] += words
                assert at[0] <= arena.shape[1], (at[0], arena.shape)
                if dt != F32:
                    v = v.bitcast(dt)
                if len(shape) > 1:
                    names = "abcde"[:len(shape)]
                    v = v.rearrange(f"p ({' '.join(names)}) -> p {' '.join(names)}",
                                    **{k: s for k, s in zip(names, shape)})
                return v
            return take

        PS = ctx.enter_context(nc.psum_tensor("PS", [P, 8, 512], F32))

        z_arena = sb("z_arena", [P, 4 * NCH * P // 2])
        take = carve(z_arena)
        Zhi, Zlo = take([NCH, P], F16), take([NCH, P], F16)
        ZThi, ZTlo = take([NCH * P], F16), take([NCH * P], F16)
        take = carve(z_arena)
        xfT = take([T])
        xfhi, xflo = take([T], F16), take([T], F16)
        hhi, hlo = take([2, 4, QB], F16), take([2, 4, QB], F16)
        gcl, sil, hid = take([RING, QB]), take([RING, QB]), take([RING, QB])
        xf = take([TC, D])
        lg, pr, cb, cb2 = (take([TC, E]) for _ in range(4))
        mx8, ix8, ixf = take([TC, 8]), take([TC, 8], U32), take([TC, 8])

        p_arena = sb("p_arena", [P, CC * P])
        take = carve(p_arena)
        ctx_sb = take([CC, P])
        take = carve(p_arena)
        Phi, Plo = take([3, 2 * QB], F16), take([3, 2 * QB], F16)
        P32 = take([2, 2 * QB])
        U_sb = take([2, QB])
        take = carve(p_arena)
        brow = take([H * D])
        Wq = take([H * D])
        bsel = take([3, 2, P])

        a_arena = sb("a_arena", [P, 4 * 4 * QB // 2])
        take = carve(a_arena)
        take([4 * QB // 2])
        Wkv, Wo = take([2 * H * D]), take([H, D])
        take = carve(a_arena)
        A = take([4, 4, QB], F16)

        w_arena = sb("w_arena", [P, 15744])
        take = carve(w_arena)
        GUhi, GUlo = take([E, 2 * F], F16), take([E, 2 * F], F16)
        DNhi, DNlo = take([E, 4, D], F16), take([E, 4, D], F16)
        SGhi, SGlo = take([2 * FS], F16), take([2 * FS], F16)
        SDhi, SDlo = take([D], F16), take([D], F16)
        stage = take([2, 2 * F + 4 * D])
        take = carve(w_arena)
        x_sb = take([TC, D])
        xT2 = take([2, T + 3])
        iw, iwk = take([2, 4, HD]), take([2, 3, 4, HD])
        WcT, WzT, WdT = take([2, 3, 2, P]), take([2, P]), take([2, 2])
        iwdt = take([2, HD])
        yo = take([2, TC, D + 1])
        ow, opw, opT, Wout = take([P]), take([P]), take([P]), take([2, P])
        zs, xc, Bc, Cc = take([2, P]), take([2, P]), take([2, P]), take([2, P])
        LT, Dec, Mt, CD, dg = (take([2, 2, P]) for _ in range(5))
        Xp, Hp = take([2, 3 * P]), take([2, 3 * P])
        yg, sq = take([2, P]), take([2, P])

        ah_arena = sb("ah_arena", [P, H * 2 * D])
        take = carve(ah_arena)
        AHhi, AHlo = take([H, 2, D], F16), take([H, 2, D], F16)
        take = carve(ah_arena)
        xs2 = take([TC, 2, 2, HD])
        VO = sb("VO", [P, H, 2, D + 2])
        WT = sb("WT", [P, 2, 5 * P])
        AH32 = sb("AH32", [P, 2, D])
        acc = sb("acc", [P, TC, D])
        m_arena = sb("m_arena", [P, T])
        take = carve(m_arena)
        Bm, Xw, y1 = take([2, P]), take([2, P]), take([2, P])
        Ht = take([2, 2, HD])
        junk = y1[:, 0, :]
        R0 = sb("R0", [1, 2, QB])
        I32, J32, ones, Epat = (sb(n, [P, P]) for n in ("I32", "J32", "ones", "Epat"))
        I16 = sb("I16", [P, P], F16)
        Tm = sb("Tm", [P, 2, P])
        zer = sb("zer", [P, P])
        vecs = sb("vecs", [P, 64])
        ctxl = sb("ctxl", [LEFT, P])
        opb, boB = sb("opb", [P, D]), sb("boB", [P, D])
        dtb, Alog, Aneg = (sb(n, [P, 2, 2]) for n in ("dtb", "Alog", "Aneg"))
        dtc = sb("dtc", [P, 6, 2, TC, 2])
        st6 = sb("st6", [P, CC + 1, 6])
        mv = sb("mv", [P, CC + 1, 2])
        rs = sb("rs", [P, 4, CC + 1])
        ssx = sb("ssx", [P, TC])
        mxs = sb("mxs", [P, 4, KB])
        mcol = sb("mcol", [P, 2, 4])
        rden = sb("rden", [P, 4])
        iota8 = sb("iota8", [P, E])
        rw = sb("rw", [P, E])
        rt = sb("rt", [P, 6, TC])
        V = {n: vecs[:, i:i + 1] for i, n in enumerate(
            ["nw_f", "nw_b", "g_m", "b_m", "g_l", "b_l", "g_f", "b_f", "gw_f", "gw_b", "D_f", "D_b"])}
        cw = vecs[:, 16:40].rearrange("p (q g k) -> p q g k", q=2, g=3)
        cbias = vecs[:, 40:46].rearrange("p (q g) -> p q g", q=2)

        ld_x, ld_iw, ld_nd, ld_mw, ld_aw, ld_ctx, ld_fv = sem("ld_x"), sem("ld_iw"), sem("ld_nd"), sem("ld_mw"), sem("ld_aw"), [sem(f"ld_ctx{i}") for i in range(3)], sem("ld_fv")
        ld_st = [sem("ld_st0"), sem("ld_st1")]
        stage_used = sem("stage_used")
        consts = sem("consts")
        pool_step, dve_step = sem("pool_step"), sem("dve_step")
        sq_in, sq_out = sem("sq_in"), sem("sq_out")
        ss_x = sem("ss_x")
        xs_ready, xT_ps, xT_a, xT_v = sem("xs_ready"), sem("xT_ps"), sem("xT_a"), sem("xT_v")
        iwk_ready, w_ps, w_sb = sem("iwk_ready"), sem("w_ps"), sem("w_sb")
        op_ps, op_sb = sem("op_ps"), sem("op_sb")
        dt_ps, dt_v, dt_a = sem("dt_ps"), sem("dt_v"), sem("dt_a")
        m_init = sem("m_init")
        two = lambda n: [sem(n + "_f"), sem(n + "_b")]
        conv_done, silu_done, dg_ready, t_done, b1_read = map(two, ("conv", "silu", "dg", "tr", "b1"))
        g_done, dec_ready, cdec_ready, m_done, xw_done = map(two, ("g", "dec", "cdec", "mm", "xw"))
        y_done, y1_done, yg_done, sq_done, out_done = map(two, ("y", "y1", "yg", "sq", "outm"))
        out_evac, s_done, ht_done, h_done = map(two, ("oev", "s", "ht", "h"))
        yo_ready, J_ps = sem("yo_ready"), sem("J_ps")
        zl_ready, zlT_ps, zlT_a, zlT_v = sem("zl_ready"), sem("zlT_ps"), sem("zlT_a"), sem("zlT_v")
        zc_ready, z_scaled, z_ones, z_hi, z_lo = sem("zc_ready"), sem("z_scaled"), sem("z_ones"), sem("z_hi"), sem("z_lo")
        zt_ps, zt_hi, zt_lo = sem("zt_ps"), sem("zt_hi"), sem("zt_lo")
        zt_lo_v = sem("zt_lo_v")
        bsel_ready, ld_b = sem("bsel_ready"), sem("ld_b")
        t_ready, wt_ps, wt_sb, ah_ps, ah_sb = sem("t_ready"), sem("wt_ps"), sem("wt_sb"), sem("ah_ps"), sem("ah_sb")
        ah_f32, ah_lo = sem("ah_f32"), sem("ah_lo")
        a_ps, a_hi, a_lo, r0_done = sem("a_ps"), sem("a_hi"), sem("a_lo"), sem("r0_done")
        mx_done, mx_read, m_col, m_neg, m_row = sem("mx_done"), sem("mx_read"), sem("m_col"), sem("m_neg"), sem("m_row")
        row_sum, row_hi, row_lo = sem("row_sum"), sem("row_hi"), sem("row_lo")
        qk_done, hi_ready, p32_ready, lo_ready = sem("qk_done"), sem("hi_ready"), sem("p32_ready"), sem("lo_ready")
        pv_done, u_evac, o_ps, o_rd, o_acc = sem("pv_done"), sem("u_evac"), sem("o_ps"), sem("o_rd"), sem("o_acc")
        w_scaled, w_head = sem("w_scaled"), sem("w_head")
        xf_ready, xfT_ps, xfT_v, xf_hi, xf_lo = sem("xf_ready"), sem("xfT_ps"), sem("xfT_v"), sem("xf_hi"), sem("xf_lo")
        rt_ps, rt_v, rt_a, comb_ready = sem("rt_ps"), sem("rt_v"), sem("rt_a"), sem("comb_ready")
        f_gate, f_up, f_clip, f_silu, f_hid, f_hi, f_lo = (sem(n) for n in ("f_gate", "f_up", "f_clip", "f_silu", "f_hid", "f_hi", "f_lo"))
        dn_ps, dn_acc = sem("dn_ps"), sem("dn_acc")
        fin, stored = sem("fin"), sem("stored")

        block = ctx.enter_context(nc.Block())

        def xp_blocks(t, q):
            return t[:, q].rearrange("p (h n) -> p h n", h=2)[:, :, 0:HD]

        def bcast_row(v, n):
            return v.rearrange("(o d) -> o d", o=1).to_broadcast([n, v.shape[0]])

        def col(v):
            return v.rearrange("(d o) -> d o", o=1)

        def loads(eng, s, pairs):
            for dst, src in pairs:
                eng.dma_start(dst, src).then_inc(s, 16)
            return 16 * len(pairs)

        dirs = [a["f"], a["b"]]
        in_w, nw_dt, mw = [], [], []
        for q, m in enumerate(dirs):
            lo, hi = HD * q, HD * q + HD
            in_w += [(iw[:, q], m["in_w"][0:4 * P, :].rearrange("(g p) d -> p g d", p=P)),
                     (iwdt[0:2, q], m["in_w"][4 * P:4 * P + 2, :]),
                     (cw[:, q], m["conv_w"].rearrange("(g p) k -> p g k", p=P))]
            mw += [*((cbias[:, q, g:g + 1], col(m["conv_b"][g * P:(g + 1) * P])) for g in range(3)),
                   (V["gw_" + "fb"[q]], col(m["gnorm_w"])),
                   (ow[lo:hi, :], m["outp_w"])]
            nw_dt += [(dtb[:, q], bcast_row(m["dt_bias"], P)), (Alog[:, q], bcast_row(m["A_log"], P))]
            nw_dt += [(V["nw_" + "fb"[q]][r:r + HD], col(a["norm_w"][lo:hi])) for r in (0, HD)]
            mw += [(V["D_" + "fb"[q]][HD * h:HD * h + HD], bcast_row(m["D"][h:h + 1], HD)) for h in (0, 1)]
        mw += [(opw, a["op_w"]), (opb[:], bcast_row(a["op_b"], P))]
        N_IW, N_ND, N_MW = (16 * len(x) for x in (in_w, nw_dt, mw))
        aw = [(V["g_m"], col(a["gamma_media"])), (V["b_m"], col(a["beta_media"])),
              (V["g_l"], col(a["gamma_lat"])), (V["b_l"], col(a["beta_lat"])),
              (Wkv, a["Wkv"]), (Wo, a["Wo"].rearrange("(h e) n -> e h n", e=D)),
              (boB[:], bcast_row(a["bo"], P))]
        N_AW = 16 * len(aw)
        ctx_rows = a["ctx"][0, 0:CC * P, :].rearrange("(p c) d -> p c d", c=CC)
        CT_PARTS = [range(0, CC // 2), range(CC // 2, CC)]
        ct = [(ctx_sb[:, r.start:r.stop], ctx_rows[:, r.start:r.stop]) for r in CT_PARTS]
        ct.append((ctxl[:], a["ctx"][0, CC * P:CTX, :]))
        fv = [(V["g_f"], col(a["ln_gamma"])), (V["b_f"], col(a["ln_beta"])), (rw[:], a["router_w"])]
        N_FV = 16 * len(fv)

        xr = a["x"][0].rearrange("(c p) d -> p c d", p=P)
        outr = out[0].rearrange("(c p) d -> p c d", p=P)

        KV_GROUPS = [(CTX0 + g, min(4, NCH - CTX0 - g)) for g in range(0, CC, 4)]

        HIW = CC // (TC - 1)
        CC_REST = CC - HIW * (TC - 1)
        HI_PARTS = [(CC - CC_REST, CC_REST)] + [(HIW * i, HIW) for i in range(TC - 1)]
        N_HI = len(HI_PARTS) + 1
        BIAS_AFTER = 2 + -(-22 // HIW)
        EARLY = 4

        ROOT_AT = 1
        DVE_AT = 4
        LAT_AT = 8

        def W_BANKS(h):
            return (2 + h % 2 * 2, 3 + h % 2 * 2, 6 + h % 2) if h < EARLY else (6, 7, 7)

        def stage_parts(par, dst):
            piece = 256
            at = 0
            for hi, lo in (dst[0:2], dst[2:4]):
                if len(hi.shape) == 3:
                    hi, lo = (x.rearrange("p i d -> p (i d)") for x in (hi, lo))
                for o in range(0, hi.shape[1], piece):
                    w = min(piece, hi.shape[1] - o)
                    yield stage[:, par, at:at + w], hi[:, o:o + w], lo[:, o:o + w]
                    at += w

        @block.sync
        def _(sp):
            sp.dma_start(x_sb, xr).then_inc(ld_x, 16)
            loads(sp, ld_iw, in_w)
            for k, (s_part, part) in enumerate(zip(ld_ctx, ct)):
                if k == 1:
                    loads(sp, ld_nd, nw_dt)
                sp.dma_start(*part).then_inc(s_part, 16)
            loads(sp, ld_mw, mw)
            loads(sp, ld_aw, aw)
            loads(sp, ld_fv, fv)
            sp.wait_ge(z_lo, BIAS_AFTER)
            sp.dma_start(Wq, a["Wq"]).then_inc(ld_b, 16)
            sp.dma_start(brow[0:1, :], bcast_row(a["bq"], 1)).then_inc(ld_b, 16)
            sp.dma_start(brow[1:3, :], a["bkv"].rearrange("(r n) -> r n", r=2)).then_inc(ld_b, 16)
            sp.wait_ge(zlT_v, 2)
            sp.wait_ge(z_lo, N_HI + 1)
            for e in range(E + 1):
                if e >= 2:
                    sp.wait_ge(stage_used, NPART * (e - 1))
                b = stage[:, e % 2]
                if e < E:
                    sp.dma_start(b[:, 0:2 * F], a["gate_up_w"][e]).then_inc(ld_st[e % 2], 16)
                    sp.dma_start(b[:, 2 * F:].rearrange("p (i d) -> p i d", i=4),
                                 a["down_w"][e].rearrange("(i p) d -> p i d", p=P)).then_inc(ld_st[e % 2], 16)
                else:
                    sp.dma_start(b[:, 0:2 * FS], a["shared_gate_up_w"]).then_inc(ld_st[e % 2], 16)
                    sp.dma_start(b[:, 2 * FS:2 * FS + D], a["shared_down_w"]).then_inc(ld_st[e % 2], 16)
            for c in range(TC):
                sp.wait_ge(fin, c + 1)
                sp.dma_start(outr[:, c, :], xf[:, c, :]).then_inc(stored, 16)
            sp.wait_ge(stored, 16 * TC)

        @block.gpsimd
        def _(pool):
            g = nc.gpsimd
            n = [0]

            def settle(ins):
                n[0] += 1
                ins.then_inc(pool_step, 1)
                pool.wait_ge(pool_step, n[0])

            g.memset(J32[:], 0.0)
            g.memset(ones[:], 1.0)
            g.memset(zer[:], 0.0)
            settle(g.memset(I32[:], 0.0))
            g.iota(iota8[:], [[1, E]], base=0, channel_multiplier=0, allow_small_or_imprecise_dtypes=True)
            g.affine_select(out=J32[:], in_=J32[:], compare_op=ALU.not_equal, fill=1.0, base=1 - P,
                            pattern=[[1, P]], channel_multiplier=1)
            settle(g.affine_select(out=I32[:], in_=I32[:], compare_op=ALU.not_equal, fill=1.0, base=0,
                                   pattern=[[-1, P]], channel_multiplier=1))
            g.tensor_copy(I16[:], I32[:])
            settle(g.tensor_copy(Epat[:], I32[:]))
            g.memset(Epat[0:1, 1:P], -1.0)
            g.memset(Xp.rearrange("p q n -> p (q n)"), 0.0)
            g.memset(Hp.rearrange("p q n -> p (q n)"), 0.0)
            g.memset(xT2.rearrange("p q n -> p (q n)"), 0.0)
            g.memset(Zhi[:, 0, :], 0.0)
            g.memset(Zlo[:, 0, :], 0.0)
            g.memset(ZThi[:, 0:P], 0.0)
            g.memset(ZTlo[:, 0:P], 0.0)
            g.memset(VO[:], 0.0).then_inc(consts, 1)

            pool.wait_ge(ld_iw, N_IW)
            for q in range(2):
                for r in range(3):
                    last = g.tensor_tensor(iwk[:, q, r], iw[:, q, 1 + r].unsqueeze(1).to_broadcast([P, 4, HD]),
                                           cw[:, q, r].unsqueeze(2).to_broadcast([P, 4, HD]), ALU.mult)
            last.then_inc(iwk_ready, 1)

            pool.wait_ge(zc_ready, 1)
            g.memset(ctx_sb[:, :, 0:1], ZS)
            g.memset(ctxl[:, 0:1], ZS)
            g.tensor_scalar(ctxl[:, 1:P], ctxl[:, 1:P], mv[0:LEFT, CC, 0:1], rs[0:LEFT, 3, CC:CC + 1],
                            ALU.subtract, ALU.mult).then_inc(z_scaled, 1)
            for c in [*range(CC - CC_REST, CC), *range(CC - CC_REST)]:
                g.tensor_scalar(ctx_sb[:, c, 1:P], ctx_sb[:, c, 1:P], mv[:, c, 0:1], rs[:, 3, c:c + 1],
                                ALU.subtract, ALU.mult).then_inc(z_scaled, 1)
            pool.wait_ge(z_hi, 1)
            g.tensor_tensor(Zlo[0:LEFT, 0, :], ctxl[:], Zhi[0:LEFT, 0, :], ALU.subtract).then_inc(z_lo, 1)
            for i, (c0, w) in enumerate(HI_PARTS):
                pool.wait_ge(z_hi, i + 2)
                g.tensor_tensor(Zlo[:, CTX0 + c0:CTX0 + c0 + w, :], ctx_sb[:, c0:c0 + w, :],
                                Zhi[:, CTX0 + c0:CTX0 + c0 + w, :], ALU.subtract).then_inc(z_lo, 1)
                if i + 2 == BIAS_AFTER:
                    pool.wait_ge(z_lo, BIAS_AFTER)
                    settle(g.memset(bsel.rearrange("p r g n -> p (r g n)"), 0.0))
                    for r in range(3):
                        last = g.tensor_copy(bsel[:, r, :, 0:1], I32[:, r:r + 1].unsqueeze(1).to_broadcast([P, 2, 1]))
                    last.then_inc(bsel_ready, 1)

            def score_matrix_low(h):
                pool.wait_ge(ah_f32, h + 1)
                pool.wait_ge(ah_sb, 2 * h + 1)
                g.tensor_tensor(AHlo[:, h], AH32[:], AHhi[:, h], ALU.subtract).then_inc(ah_lo, 1)

            for h in range(EARLY):
                score_matrix_low(h)

            pool.wait_ge(zl_ready, 1)
            g.memset(x_sb[:, :, 0:1], ZS).then_inc(z_ones, 1)
            pool.wait_ge(z_ones, 1)
            g.tensor_copy(Zhi[:, LAT0:CTX0, :], x_sb).then_inc(z_hi, 1)
            pool.wait_ge(z_hi, N_HI + 1)
            g.tensor_tensor(Zlo[:, LAT0:CTX0, :], x_sb, Zhi[:, LAT0:CTX0, :], ALU.subtract).then_inc(z_lo, 1)

            for h in range(EARLY, H):
                score_matrix_low(h)

            for e in range(E + 1):
                pool.wait_ge(ld_st[e % 2], 32 * (e // 2) + 32)
                pairs = (GUhi[:, e], GUlo[:, e], DNhi[:, e], DNlo[:, e]) if e < E else (SGhi, SGlo, SDhi, SDlo)
                for k, (src, hi, lo) in enumerate(stage_parts(e % 2, pairs)):
                    n_piece = NPART * e + k + 1
                    g.tensor_scalar(src, src, WS, 0.0, ALU.mult, ALU.add).then_inc(w_scaled, 1)
                    pool.wait_ge(w_scaled, n_piece)
                    g.tensor_copy(hi, src).then_inc(w_head, 1)
                    pool.wait_ge(w_head, n_piece)
                    g.tensor_tensor(lo, src, hi, ALU.subtract).then_inc(stage_used, 1)

            def hidden_low(u, k, half, i):
                pool.wait_ge(f_hi, u + 1)
                g.tensor_tensor(hlo[:, half, i], hid[:, k % RING], hhi[:, half, i], ALU.subtract).then_inc(f_lo, 1)

            for k in range(8):
                hidden_low(k, k, k // 4, k % 4)
            with pool.Fori(1, E) as e:
                for k in range(8):
                    hidden_low(8 * e + k, k, k // 4, k % 4)
            for half in range(2):
                hidden_low(8 * E + half, half, half, 0)

        @block.scalar
        def _(act):
            s = nc.scalar

            def root(k):
                act.wait_ge(sq_in, k)
                s.activation(rs[:, 1, :], rs[:, 0, :], ACT.Sqrt).then_inc(sq_out, 1)

            act.wait_ge(ld_x, 16)
            for c in range(TC):
                if c:
                    act.wait_ge(ss_x, c)
                s.activation(junk, x_sb[:, c, :], ACT.Square, accum_out=ssx[:, c:c + 1]).then_inc(ss_x, 1)
            root(1)
            act.wait_ge(xT_ps, 2 * TC)
            act.wait_ge(consts, 1)
            for q in range(2):
                s.copy(xT2[0:HD, q, 3:3 + T].rearrange("p (b n) -> p b n", b=2),
                       PS[0:HD, 2 * q:2 * q + 2, :]).then_inc(xT_a, 1)
            act.wait_ge(dt_v, 1)
            s.activation(dtc[:, 1], dtc[:, 1], ACT.Exp).then_inc(dt_a, 1)
            s.activation(Aneg[:], Alog[:], ACT.Exp).then_inc(dt_a, 1)
            act.wait_ge(dt_v, 2)
            s.activation(dtc[:, 3], dtc[:, 2], ACT.Ln).then_inc(dt_a, 1)
            act.wait_ge(dt_v, 5)
            s.activation(dtc[:, 5], dtc[:, 4], ACT.Exp).then_inc(dt_a, 1)
            root(2)
            s.activation(rt[:, 5, 0:1], iota8[:, 0:1], ACT.Silu)
            def silus(c, q):
                act.wait_ge(conv_done[q], c + 1)
                s.activation(zs[:, q], PS[:, 4 * q, 0:P], ACT.Silu).then_inc(silu_done[q], 1)
                for r, t in enumerate((xc, Bc, Cc)):
                    s.activation(t[:, q], PS[:, 4 * q, (r + 1) * P:(r + 2) * P], ACT.Silu,
                                 bias=cbias[:, q, r:r + 1]).then_inc(silu_done[q], 1)

            def chunk_act(c, last_one=False):
                for q in range(2):
                    act.wait_ge(yg_done[q], c + 1)
                    s.activation(sq[:, q], yg[:, q], ACT.Square).then_inc(sq_done[q], 1)
                    if not last_one:
                        silus(c + 1, q)
                for q in range(2):
                    act.wait_ge(out_done[q], c + 1)
                    at = c if q == 0 else (TC - 1) - c
                    s.copy(yo[:, q, at, :], PS[:, 4 * q + 3, P:2 * P + 1]).then_inc(out_evac[q], 1)
                if not last_one:
                    act.wait_ge(z_scaled, HIW * c + (HIW + 1 + CC_REST))
                    s.copy(Zhi[:, bass.ds(CTX0 + HIW * c, HIW), :], ctx_sb[:, bass.ds(HIW * c, HIW), :]).then_inc(z_hi, 1)

            act.wait_ge(z_scaled, 1 + CC_REST)
            s.copy(Zhi[0:LEFT, 0, :], ctxl[:]).then_inc(z_hi, 1)
            s.copy(Zhi[:, NCH - CC_REST:NCH, :], ctx_sb[:, CC - CC_REST:CC, :]).then_inc(z_hi, 1)
            for q in range(2):
                silus(0, q)
            with act.Fori(0, TC - 1) as c:
                chunk_act(c)
            chunk_act(TC - 1, last_one=True)
            root(3)
            def head_act(h):
                act.wait_ge(wt_ps, 2 * h + 1)
                if h >= 2:
                    act.wait_ge(ah_ps, h - 1)
                s.copy(WT[:, h % 2, 0:3 * P], PS[:, W_BANKS(h)[0], 0:3 * P]).then_inc(wt_sb, 1)
                act.wait_ge(wt_ps, 2 * h + 2)
                s.copy(WT[:, h % 2, 3 * P:5 * P], PS[:, W_BANKS(h)[1], 0:2 * P]).then_inc(wt_sb, 1)
                act.wait_ge(ah_ps, h + 1)
                b = PS[:, W_BANKS(h)[2], :].rearrange("p (k g d) -> p k g d", k=2, g=2)
                scale = AHS * AS / ZS * float(D) ** -0.5
                if h:
                    act.wait_ge(ah_lo, h)
                s.activation(AH32[:], b[:, 0], ACT.Copy, scale=scale).then_inc(ah_f32, 1)
                s.activation(AHhi[:, h], b[:, 0], ACT.Copy, scale=scale).then_inc(ah_sb, 1)
                s.copy(VO[:, h, :, 0:D], b[:, 1]).then_inc(ah_sb, 1)

            for h in range(EARLY):
                if h == 1:
                    root(4)
                head_act(h)
            def latents_act():
                for i in range(2):
                    act.wait_ge(zlT_ps, 4 * i + 4)
                    s.copy(ZThi[:, LAT0 * P + i * QB:LAT0 * P + (i + 1) * QB], PS[:, i, :]).then_inc(zlT_a, 1)

            for i, (c0, w) in enumerate(KV_GROUPS + [(0, 1)]):
                if i == ROOT_AT:
                    root(5)
                if i == LAT_AT:
                    latents_act()
                n = w * P if c0 else LEFT
                for o, (dst, done) in enumerate(((ZThi, zt_hi), (ZTlo, zt_lo))[:2 if i < DVE_AT else 1]):
                    act.wait_ge(zt_ps, 2 * i + o + 1)
                    s.copy(dst[:, c0 * P:c0 * P + n], PS[:, 2 + 2 * (i % 2) + o, 0:n]).then_inc(done, 1)

            def a_high(b):
                for g in range(2):
                    act.wait_ge(a_ps, 2 * b + g + 1)
                    s.activation(A[:, b % 4, 2 * g, :], PS[:, 7 - g, :], ACT.Copy, scale=1 / AHS).then_inc(a_hi, 1)

            def weights(j, st):
                g, (r, _) = step_number(j, st), place_of(st)
                w = len(STEPS[r]) * QB
                ps = PS[:, 2 * (r % 2):2 * (r % 2) + 2, :].rearrange("p b n -> p (b n)")[:, 0:w]
                act.wait_ge(qk_done, g + 1)
                if not early(j, st, 3):
                    act.wait_ge(pv_done, g - 2)
                s.activation(Phi[:, r % 3, 0:w], ps, ACT.Exp, scale=1 / SSC).then_inc(hi_ready, 1)
                if not early(j, st, 2):
                    act.wait_ge(lo_ready, g - 1)
                s.activation(P32[:, r % 2, 0:w], ps, ACT.Exp, scale=1 / SSC).then_inc(p32_ready, 1)

            def evac(j):
                act.wait_ge(pv_done, NS * j + NS)
                if not (isinstance(j, int) and j == 0):
                    act.wait_ge(o_ps, 2 * j)
                s.copy(U_sb, PS[:, 4:6, :]).then_inc(u_evac, 1)

            def block_act(j, first=False, nxt=True):
                for st in range(LOOP0):
                    weights(j, st)
                    if st == 1 and not first:
                        evac(j - 1)
                with act.Fori(0, LOOPN) as i:
                    for k in range(6):
                        weights(j, Turn(i, k))
                for st in range(TAIL, NS):
                    weights(j, st)
                    if st == NS - 2 and nxt:
                        a_high(j + 2)

            a_high(0)
            for h in range(EARLY, H):
                head_act(h)
            a_high(1)
            s.activation(rt[:, 5, 0:1], iota8[:, 0:1], ACT.Exp)
            block_act(0, first=True)
            with act.Fori(1, NBLK - 2) as j:
                block_act(j)
            block_act(NBLK - 2, nxt=False)
            block_act(NBLK - 1, nxt=False)
            evac(NBLK - 1)

            root(6)
            root(7)
            act.wait_ge(xfT_v, 2)
            s.activation(xfhi, xfT, ACT.Copy, scale=XS).then_inc(xf_hi, 1)
            act.wait_ge(rt_v, 1)
            for c in range(TC):
                s.activation(pr[:, c], lg[:, c], ACT.Exp, bias=rt[:, 0, c:c + 1],
                             accum_out=rt[:, 1, c:c + 1]).then_inc(rt_a, 1)
            s.activation(rt[:, 5, 0:1], iota8[:, 0:1], ACT.Silu)

            def silu(u, k):
                act.wait_ge(f_clip, u + 1)
                if not (isinstance(u, int) and u < RING):
                    act.wait_ge(f_hid, u + (1 - RING))
                s.activation(sil[:, k % RING], gcl[:, k % RING], ACT.Silu, scale=1 / (XS * WS)).then_inc(f_silu, 1)

            def high(u, k, g2, i, first):
                act.wait_ge(f_hid, u + 1)
                if not first:
                    act.wait_ge(dn_ps, 4 * g2 - 4)
                s.copy(hhi[:, k // 4 % 2, i], hid[:, k % RING]).then_inc(f_hi, 1)

            def expert_act(e, first=False):
                for k in range(8):
                    silu(8 * e + k, k)
                    if not (first and k == 0):
                        p = (k - 1) % 8
                        high(8 * e + (k - 1), p, 2 * e + (-1 if k == 0 else p // 4), p % 4, first)

            expert_act(0, first=True)
            with act.Fori(1, E) as e:
                expert_act(e, first=False)
            silu(8 * E, 0)
            high(8 * E - 1, 7, 2 * E - 1, 3, False)
            silu(8 * E + 1, 1)
            act.wait_ge(f_hid, 8 * E + 1)
            act.wait_ge(dn_ps, 8 * E - 4)
            s.copy(hhi[:, 0, 0], hid[:, 0]).then_inc(f_hi, 1)
            act.wait_ge(f_hid, 8 * E + 2)
            act.wait_ge(dn_ps, 8 * E)
            s.copy(hhi[:, 1, 0], hid[:, 1]).then_inc(f_hi, 1)
            root(8)

        @block.vector
        def _(dve):
            v = nc.vector
            n = [0]

            def settle(ins):
                n[0] += 1
                ins.then_inc(dve_step, 1)
                dve.wait_ge(dve_step, n[0])

            def inv_root(k, w, var, mul=1.0, add=EPS):
                v.tensor_scalar(rs[:, 0, 0:w], var, mul, add, ALU.mult, ALU.add).then_inc(sq_in, 1)
                dve.wait_ge(sq_in, k)
                dve.wait_ge(sq_out, k)
                settle(v.reciprocal(rs[:, 3, 0:w], rs[:, 1, 0:w]))
                settle(v.tensor_tensor(rs[:, 1, 0:w], rs[:, 3, 0:w], rs[:, 3, 0:w], ALU.mult))
                settle(v.tensor_tensor(rs[:, 1, 0:w], rs[:, 1, 0:w], rs[:, 0, 0:w], ALU.mult))
                settle(v.tensor_scalar(rs[:, 1, 0:w], rs[:, 1, 0:w], -0.5, 1.5, ALU.mult, ALU.add))
                settle(v.tensor_tensor(rs[:, 3, 0:w], rs[:, 3, 0:w], rs[:, 1, 0:w], ALU.mult))

            settle(v.memset(rs[:], 1.0))
            settle(v.memset(mv[:], 1.0))
            dve.wait_ge(ss_x, TC)
            inv_root(1, TC, ssx[:], 1.0 / D)
            for c in range(TC):
                last = v.tensor_scalar(xs2[:, c], x_sb[:, c].rearrange("p (q d) -> p q d", q=2).unsqueeze(2)
                                       .to_broadcast([P, 2, 2, HD]), rs[:, 3, c:c + 1], None, ALU.mult)
                last.then_inc(xs_ready, 1)
            dve.wait_ge(ld_ctx[0], 16)
            for c in CT_PARTS[0]:
                v.bn_stats(st6[:, c, :], ctx_sb[:, c, :])
            dve.wait_ge(consts, 1)
            dve.wait_ge(xT_ps, 2 * TC)
            for q in range(2):
                v.tensor_copy(xT2[HD:P, q, 2:2 + T].rearrange("p (b n) -> p b n", b=2),
                              PS[HD:P, 2 * q:2 * q + 2, :]).then_inc(xT_v, 1)
            dve.wait_ge(ld_nd, N_ND)
            dve.wait_ge(w_ps, 1)
            for q in range(2):
                nw = V["nw_" + "fb"[q]]
                v.tensor_scalar(WcT[:, q, 0:2].rearrange("p g k c -> p (g k c)"), PS[:, 4 + 2 * q, :], nw, None, ALU.mult)
                v.tensor_scalar(WcT[:, q, 2].rearrange("p k c -> p (k c)"), PS[:, 5 + 2 * q, 0:2 * P], nw, None, ALU.mult)
                v.tensor_scalar(WzT[0:HD, q], PS[0:HD, 5 + 2 * q, 2 * P:3 * P], nw[0:HD], None, ALU.mult)
                v.tensor_scalar(WdT[0:HD, q], PS[0:HD, 5 + 2 * q, 3 * P:3 * P + 2], nw[0:HD], None,
                                ALU.mult).then_inc(w_sb, 1)
            dve.wait_ge(ld_ctx[1], 16)
            for c in CT_PARTS[1]:
                v.bn_stats(st6[:, c, :], ctx_sb[:, c, :])
            dve.wait_ge(ld_ctx[2], 16)
            settle(v.bn_stats(st6[0:LEFT, CC, :], ctxl[:]))
            dve.wait_ge(dt_ps, 1)
            bc = lambda t: t[:].unsqueeze(2).to_broadcast([P, 2, TC, 2])
            settle(v.tensor_tensor(dtc[:, 0], PS[:, 0, 0:4 * TC].rearrange("p (q c h) -> p q c h", q=2, c=TC), bc(dtb), ALU.add))
            fl = [dtc[:, i].rearrange("p q c h -> p (q c h)") for i in range(6)]
            v.scalar_tensor_tensor(out=fl[1], in0=fl[0], scalar=-1.0, in1=fl[0], op0=ALU.mult,
                                   op1=ALU.min).then_inc(dt_v, 1)
            for c in range(CC):
                v.bn_aggr(mv[:, c, :], st6[:, c, :])
            settle(v.bn_aggr(mv[0:LEFT, CC, :], st6[0:LEFT, CC, :]))
            dve.wait_ge(dt_a, 1)
            v.tensor_scalar(fl[2], fl[1], 1.0, None, ALU.add).then_inc(dt_v, 1)
            dve.wait_ge(dt_v, 2)
            dve.wait_ge(dt_a, 3)
            settle(v.tensor_scalar(fl[4], fl[2], -1.0, 1e-30, ALU.add, ALU.max))
            settle(v.reciprocal(fl[4], fl[4]))
            settle(v.tensor_tensor(fl[3], fl[3], fl[4], ALU.mult))
            settle(v.tensor_scalar(fl[4], fl[2], 1.0, None, ALU.is_equal))
            settle(v.tensor_tensor(fl[3], fl[3], fl[4], ALU.add))
            settle(v.tensor_tensor(fl[3], fl[3], fl[1], ALU.mult))
            v.scalar_tensor_tensor(out=fl[3], in0=fl[0], scalar=0.0, in1=fl[3], op0=ALU.max,
                                   op1=ALU.add).then_inc(dt_v, 1)
            v.tensor_scalar(Aneg[:], Aneg[:], -1.0, None, ALU.mult).then_inc(dt_v, 1)
            dve.wait_ge(dt_v, 4)
            v.tensor_tensor(dtc[:, 4], dtc[:, 3], bc(Aneg), ALU.mult).then_inc(dt_v, 1)
            dve.wait_ge(ld_aw, N_AW)
            for g, k in enumerate("ml"):
                settle(v.tensor_scalar(Tm[:, g], Epat[:], V["g_" + k], None, ALU.mult))
                v.tensor_copy(Tm[:, g, 0:1], V["b_" + k]).then_inc(t_ready, 1)
            for h in range(H):
                last = v.tensor_copy(VO[:, h, :, D:D + 1], I32[:, 0:1].unsqueeze(1).to_broadcast([P, 2, 1]))
            last.then_inc(t_ready, 1)
            inv_root(2, CC + 1, mv[:, :, 1])
            v.tensor_scalar(rs[:, 3], rs[:, 3], ZS, None, ALU.mult).then_inc(zc_ready, 1)

            dve.wait_ge(ld_mw, N_MW)
            dve.wait_ge(op_ps, 1)
            v.tensor_copy(opT, PS[:, 3, 0:P]).then_inc(op_sb, 1)
            dve.wait_ge(op_ps, 2)
            for q in range(2):
                v.tensor_scalar(Wout[:, q], PS[:, 1 + q, 0:P], V["gw_" + "fb"[q]], None,
                                ALU.mult).then_inc(op_sb, 1)

            def diagonals(q, c):
                v.tensor_tensor(dg[:, q], I32[:].unsqueeze(1).to_broadcast([P, 2, P]),
                                dtc[:, 5, q, c, :].unsqueeze(2).to_broadcast([P, 2, P]),
                                ALU.mult).then_inc(dg_ready[q], 1)

            def chunk_dve(c, last_one=False):
                for q in range(2):
                    b1 = PS[:, 4 * q + 1]
                    dve.wait_ge(t_done[q], c + 1)
                    for h in range(2):
                        last = v.tensor_tensor_scan(Dec[:, q, h], b1[:, (2 + h) * P:(3 + h) * P], zer[:], 1.0,
                                                    ALU.mult, ALU.add)
                    last.then_inc(dec_ready[q], 1)
                    if not last_one:
                        diagonals(q, c + 1)
                    for h in range(2):
                        v.tensor_tensor_scan(LT[:, q, h], b1[:, (2 + h) * P:(3 + h) * P], I32[:], 0.0,
                                             ALU.mult, ALU.add)
                    after(dve, y_done[q], c)
                    after(dve, s_done[q], c)
                    v.tensor_tensor(xp_blocks(Xp, q), b1[:, 0:P].rearrange("p (h d) -> p h d", h=2),
                                    dtc[:, 3, q, c, :].unsqueeze(2).to_broadcast([P, 2, HD]), ALU.mult)
                    v.tensor_copy(Bm[:, q], b1[:, P:2 * P]).then_inc(b1_read[q], 1)
                    dve.wait_ge(b1_read[q], c + 1)
                    v.tensor_tensor(Xw[:, q].rearrange("p (h d) -> p h d", h=2), xp_blocks(Xp, q),
                                    LT[:, q, :, P - 1:P].to_broadcast([P, 2, HD]), ALU.mult).then_inc(xw_done[q], 1)
                    dve.wait_ge(dec_ready[q], c + 1)
                    v.tensor_tensor(CD[:, q], Dec[:, q], Cc[:, q].unsqueeze(1).to_broadcast([P, 2, P]),
                                    ALU.mult).then_inc(cdec_ready[q], 1)
                    dve.wait_ge(g_done[q], c + 1)
                    v.tensor_tensor(Mt[:, q], LT[:, q], PS[:, 4 * q + 2, 0:P].unsqueeze(1).to_broadcast([P, 2, P]),
                                    ALU.mult).then_inc(m_done[q], 1)
                for q in range(2):
                    dve.wait_ge(y_done[q], c + 1)
                    v.scalar_tensor_tensor(out=y1[:, q], in0=xc[:, q], scalar=V["D_" + "fb"[q]],
                                           in1=PS[:, 4 * q + 3, 0:P], op0=ALU.mult, op1=ALU.add).then_inc(y1_done[q], 1)
                    dve.wait_ge(y1_done[q], c + 1)
                    after(dve, out_done[q], c)
                    after(dve, sq_done[q], c)
                    v.tensor_tensor(yg[:, q], y1[:, q], zs[:, q], ALU.mult).then_inc(yg_done[q], 1)
                    dve.wait_ge(s_done[q], c + 1)
                    v.tensor_tensor(Ht[:, q], xp_blocks(Hp, q), Dec[:, q, :, P - 1:P].to_broadcast([P, 2, HD]),
                                    ALU.mult).then_inc(ht_done[q], 1)
                    dve.wait_ge(ht_done[q], c + 1)
                    v.tensor_tensor(xp_blocks(Hp, q), Ht[:, q],
                                    PS[:, 4 * q + 2, P:2 * P].rearrange("p (h d) -> p h d", h=2),
                                    ALU.add).then_inc(h_done[q], 1)


            dve.wait_ge(dt_a, 4)
            for q in range(2):
                diagonals(q, 0)
            v.scalar_tensor_tensor(out=x_sb, in0=x_sb, scalar=2.0, in1=opb[:].unsqueeze(1).to_broadcast([P, TC, D]),
                                   op0=ALU.mult, op1=ALU.add)
            chunk_dve(0)
            with dve.Fori(1, TC - 1) as c:
                chunk_dve(c)
            chunk_dve(TC - 1, last_one=True)
            dve.wait_ge(z_scaled, CC + 1)
            for q in range(2):
                dve.wait_ge(out_evac[q], TC)
            inv_root(3, 2 * TC, yo[:, :, :, D:D + 1].rearrange("p q c o -> p q (c o)"), 1.0 / D)
            rsv = rs[:, 3, 0:2 * TC].rearrange("p (q c) -> p q c", q=2)
            for q in (1, 0):
                v.tensor_tensor(yo[:, q, :, 0:D], yo[:, q, :, 0:D],
                                rsv[:, q].unsqueeze(2).to_broadcast([P, TC, D]), ALU.mult).then_inc(yo_ready, 1)
            dve.wait_ge(yo_ready, 2)
            settle(v.tensor_tensor(x_sb, x_sb, yo[:, 0, :, 0:D], ALU.add))
            dve.wait_ge(J_ps, 2)
            settle(v.tensor_tensor(x_sb.rearrange("p c d -> p (c d)").rearrange("p (b n) -> p b n", b=2),
                                   x_sb.rearrange("p c d -> p (c d)").rearrange("p (b n) -> p b n", b=2),
                                   PS[:, 0:2, :], ALU.add))

            def norm_stats(t, k):
                for c in range(TC):
                    last = v.bn_stats(st6[:, c, :], t[:, c, :])
                settle(last)
                for c in range(TC):
                    last = v.bn_aggr(mv[:, c, :], st6[:, c, :])
                settle(last)
                inv_root(k, TC, mv[:, 0:TC, 1])

            def norm_rows(dst, src):
                for c in range(TC):
                    last = v.tensor_scalar(dst[:, c, :], src[:, c, :], mv[:, c, 0:1], rs[:, 3, c:c + 1],
                                           ALU.subtract, ALU.mult)
                return last

            norm_stats(x_sb, 4)
            settle(norm_rows(x_sb, x_sb))
            v.tensor_tensor(acc[:], x_sb, boB[:].unsqueeze(1).to_broadcast([P, TC, D]), ALU.add)
            norm_stats(x_sb, 5)
            settle(v.tensor_scalar(rs[:, 3, 0:TC], rs[:, 3, 0:TC], ZS, None, ALU.mult))
            norm_rows(x_sb, x_sb).then_inc(zl_ready, 1)
            for i, (c0, w) in enumerate(KV_GROUPS + [(0, 1)]):
                if i == LAT_AT:
                    for k in range(2):
                        dve.wait_ge(zlT_a, k + 1)
                        at = slice(LAT0 * P + k * QB, LAT0 * P + (k + 1) * QB)
                        v.tensor_tensor(ZTlo[:, at], PS[:, k, :], ZThi[:, at], ALU.subtract).then_inc(zlT_v, 1)
                if i >= DVE_AT:
                    dve.wait_ge(zt_ps, 2 * i + 2)
                    cols = w * P if c0 else LEFT
                    v.tensor_copy(ZTlo[:, c0 * P:c0 * P + cols], PS[:, 3 + 2 * (i % 2), 0:cols]).then_inc(zt_lo_v, 1)

            def row_zero(b):
                return U_sb[0:1] if isinstance(b, int) and b == 0 else R0[:]

            def a_low(b):
                for g in range(2):
                    dve.wait_ge(a_hi, 2 * b + g + 1)
                    v.tensor_scalar(row_zero(b)[:, g, :], PS[0:1, 7 - g, :], 1 / AHS, None, ALU.mult).then_inc(r0_done, 1)
                    v.scalar_tensor_tensor(out=A[:, b % 4, 2 * g + 1, :], in0=PS[:, 7 - g, :], scalar=1 / AHS,
                                           in1=A[:, b % 4, 2 * g, :], op0=ALU.mult, op1=ALU.subtract).then_inc(a_lo, 1)

            def unit_max(n, par, kb, i):
                dve.wait_ge(mx_done, n + 1)
                w = 2 * P + LEFT if isinstance(kb, int) and kb == KB_LEFT else QB
                v.tensor_reduce(mxs[:, i, bass.ds(kb, 1)], PS[:, 6 + par, 0:w], AX.X, ALU.max).then_inc(mx_read, 1)

            def max_column(b):
                dve.wait_ge(mx_read, NU * b + NU)
                v.tensor_reduce(mcol[:, 0, :], mxs[:], AX.X, ALU.max).then_inc(m_col, 1)
                dve.wait_ge(m_col, b + 1)
                v.tensor_scalar(mcol[:, 1, :], mcol[:, 0, :], -1.0 / ZS, LIFT * AS, ALU.mult, ALU.add).then_inc(m_neg, 1)

            def max_row(b):
                dve.wait_ge(m_row, b + 1)
                dve.wait_ge(r0_done, 2 * b + 2)
                r0 = row_zero(b)
                v.tensor_tensor(r0, r0, PS[0:1, 6, :].unsqueeze(1).to_broadcast([1, 2, QB]),
                                ALU.add).then_inc(row_sum, 1)
                pair = A[0:1, b % 4].rearrange("p (g k) n -> p g k n", g=2)
                dve.wait_ge(row_sum, b + 1)
                v.tensor_copy(pair[:, :, 0, :], r0).then_inc(row_hi, 1)
                dve.wait_ge(row_hi, b + 1)
                v.tensor_tensor(pair[:, :, 1, :], r0, pair[:, :, 0, :], ALU.subtract).then_inc(row_lo, 1)

            def low(j, st):
                g, (r, _) = step_number(j, st), place_of(st)
                w = len(STEPS[r]) * QB
                dve.wait_ge(p32_ready, g + 1)
                v.tensor_tensor(Plo[:, r % 3, 0:w], P32[:, r % 2, 0:w], Phi[:, r % 3, 0:w],
                                ALU.subtract).then_inc(lo_ready, 1)

            def project_acc(b, k):
                o = PS[:, 7 - k].rearrange("p (i n) -> p i n", n=256)
                dve.wait_ge(o_ps, 2 * b + k + 1)
                v.reciprocal(rden[:, 2 * k:2 * k + 2].unsqueeze(2), o[:, :, D:D + 1]).then_inc(o_rd, 1)
                dve.wait_ge(o_rd, 2 * b + k + 1)
                for i in range(2):
                    t = b // H * 4 + 2 * k + i
                    last = v.scalar_tensor_tensor(out=acc[:, t, :], in0=o[:, i, 0:D], scalar=rden[:, 2 * k + i:2 * k + i + 1],
                                                  in1=acc[:, t, :], op0=ALU.mult, op1=ALU.add)
                last.then_inc(o_acc, 1)

            def block_dve(j, first=False, maxes=True, nxt=True):
                b, u = j + 1, 0
                for st in range(LOOP0):
                    if maxes:
                        for _ in range(UNITS_HEAD[st]):
                            unit_max(NU * b + u, u % 2, KB_LEFT + u // 4, u % 4)
                            u += 1
                    low(j, st)
                with dve.Fori(0, LOOPN) as i:
                    u = 0
                    for k in range(6):
                        if maxes:
                            for _ in range(UNITS_TURN[k]):
                                unit_max(NU * b + 16 * i + (12 + u), u % 2, 4 * i + u // 4, u % 4)
                                u += 1
                        low(j, Turn(i, k))
                if maxes:
                    max_column(b)
                for st in range(TAIL, NS):
                    low(j, st)
                    if st == TAIL and maxes:
                        max_row(b)
                    if st in (TAIL + 1, TAIL + 2) and not first:
                        project_acc(j - 1, st - TAIL - 1)
                    if st == NS - 2 and nxt:
                        a_low(j + 2)

            a_low(0)
            for pair in range(NU // 2):
                dve.wait_ge(mx_done, 2 * pair + 2)
                kb, i = pair // 2, pair % 2 * 2
                w = 2 * P + LEFT if kb == KB_LEFT else QB
                v.tensor_reduce(mxs[:, i:i + 2, kb:kb + 1], PS[:, pair % 3 * 2:pair % 3 * 2 + 2, 0:w], AX.X,
                                ALU.max).then_inc(mx_read, 2)
                if pair == 24:
                    a_low(1)
            max_column(0)
            max_row(0)
            block_dve(0, first=True)
            with dve.Fori(1, NBLK - 2) as j:
                block_dve(j)
            block_dve(NBLK - 2, nxt=False)
            block_dve(NBLK - 1, maxes=False, nxt=False)
            project_acc(NBLK - 1, 0)
            project_acc(NBLK - 1, 1)

            dve.wait_ge(o_acc, 2 * NBLK)
            norm_stats(acc, 6)
            settle(norm_rows(acc, acc))
            norm_stats(acc, 7)
            norm_rows(xf, acc).then_inc(xf_ready, 1)
            dve.wait_ge(ld_fv, N_FV)
            for i in range(2):
                dve.wait_ge(xfT_ps, 4 * i + 4)
                v.tensor_scalar(xfT[:, i * QB:(i + 1) * QB], PS[:, i, :], V["g_f"], V["b_f"], ALU.mult,
                                ALU.add).then_inc(xfT_v, 1)
            dve.wait_ge(xf_hi, 1)
            v.scalar_tensor_tensor(out=xflo, in0=xfT, scalar=XS, in1=xfhi, op0=ALU.mult, op1=ALU.subtract).then_inc(xf_lo, 1)
            dve.wait_ge(rt_ps, 1)
            settle(v.tensor_copy(lg[:], PS[:, 2, 0:TC * E].rearrange("p (c e) -> p c e", c=TC)))
            settle(v.tensor_reduce(rt[:, 0, :].unsqueeze(2), lg[:], AX.X, ALU.max))
            v.tensor_scalar(rt[:, 0, :], rt[:, 0, :], -1.0, None, ALU.mult).then_inc(rt_v, 1)
            dve.wait_ge(rt_a, TC)
            settle(v.reciprocal(rt[:, 1, :], rt[:, 1, :]))
            settle(v.tensor_tensor(pr[:], pr[:], rt[:, 1, :].unsqueeze(2).to_broadcast([P, TC, E]), ALU.mult))
            for c in range(TC):
                last = v.max(mx8[:, c], pr[:, c])
            settle(last)
            for c in range(TC):
                last = v.max_index(ix8[:, c], mx8[:, c], pr[:, c])
            settle(last)
            settle(v.tensor_copy(ixf[:], ix8[:]))
            settle(v.tensor_tensor(rt[:, 2, :].unsqueeze(2), mx8[:, :, 0:1], mx8[:, :, 1:2], ALU.add))
            settle(v.reciprocal(rt[:, 2, :], rt[:, 2, :]))
            settle(v.tensor_scalar(rt[:, 2, :], rt[:, 2, :], 1 / (HS * WS), None, ALU.mult))
            settle(v.tensor_tensor(mx8[:, :, 0:2], mx8[:, :, 0:2],
                                   rt[:, 2, :].unsqueeze(2).to_broadcast([P, TC, 2]), ALU.mult))
            for k, dst in ((0, cb), (1, cb2)):
                settle(v.tensor_tensor(dst[:], iota8[:].unsqueeze(1).to_broadcast([P, TC, E]),
                                       ixf[:, :, k:k + 1].to_broadcast([P, TC, E]), ALU.is_equal))
                settle(v.tensor_tensor(dst[:], dst[:], mx8[:, :, k:k + 1].to_broadcast([P, TC, E]), ALU.mult))
            settle(v.tensor_tensor(cb[:], cb[:], cb2[:], ALU.add))

            def clip(u, k):
                dve.wait_ge(f_gate, u + 1)
                if not (isinstance(u, int) and u < RING):
                    dve.wait_ge(f_silu, u + (1 - RING))
                lim = 10.0 * XS * WS
                v.tensor_scalar(gcl[:, k % RING], PS[:, k % 2], lim, -lim, ALU.min, ALU.max).then_inc(f_clip, 1)

            def hidden(u, k):
                dve.wait_ge(f_silu, u + 1)
                dve.wait_ge(f_up, u + 1)
                if not (isinstance(u, int) and u < RING):
                    dve.wait_ge(f_hi, u + (1 - RING))
                    dve.wait_ge(f_lo, u + (1 - RING))
                v.scalar_tensor_tensor(out=hid[:, k % RING], in0=PS[:, 2 + k % RING], scalar=HS / (XS * WS),
                                       in1=sil[:, k % RING], op0=ALU.mult, op1=ALU.mult).then_inc(f_hid, 1)

            def down_acc(e, half, t):
                n, c = 8 * e + 4 * half + t, 4 * half + t
                dve.wait_ge(dn_ps, n + 1)
                if not (isinstance(n, int) and n < 2):
                    dve.wait_ge(dn_acc, n - 1)
                share = 1 / (HS * WS) if isinstance(e, int) and e == E else cb[:, c, bass.ds(e, 1)]
                v.scalar_tensor_tensor(out=acc[:, c, :], in0=PS[:, 6 + t % 2, 0:P], scalar=share,
                                       in1=acc[:, c, :], op0=ALU.mult, op1=ALU.add).then_inc(dn_acc, 1)

            def expert_dve(e, first=False):
                for k in range(8):
                    clip(8 * e + k, k)
                    if not (first and k < 1):
                        hidden(8 * e + (k - 1), (k - 1) % 8)
                    for m in sum(TILES[(k - 1) % 8], []):
                        own = m < 2 and k > 0
                        if own or not first:
                            down_acc(e if own else e - 1, m // 4, m % 4)

            expert_dve(0, first=True)
            with dve.Fori(1, E) as e:
                expert_dve(e)
            clip(8 * E, 0)
            hidden(8 * E - 1, 7)
            for m in (1, 2):
                down_acc(E - 1, 0, m)
            clip(8 * E + 1, 1)
            hidden(8 * E, 0)
            down_acc(E - 1, 0, 3)
            hidden(8 * E + 1, 1)
            for m in range(4, 8):
                down_acc(E - 1, m // 4, m % 4)
            for m in range(8):
                down_acc(E, m // 4, m % 4)
            dve.wait_ge(dn_acc, TC * (E + 1))
            norm_stats(acc, 8)
            for c in range(TC):
                v.tensor_scalar(xf[:, c, :], acc[:, c, :], mv[:, c, 0:1], rs[:, 3, c:c + 1],
                                ALU.subtract, ALU.mult).then_inc(fin, 1)

        @block.tensor
        def _(pe):
            t = nc.tensor

            def mm(o, l, r, start=True, stop=True):
                return t.matmul(o, l, r, start=start, stop=stop)

            pe.wait_ge(consts, 1)
            for c in range(TC):
                pe.wait_ge(xs_ready, c + 1)
                for q in range(2):
                    at = c if q == 0 else TC - 1 - c
                    mm(PS[:, 2 * q + at // 4, at % 4 * P:(at % 4 + 1) * P], xs2[:, c, q].rearrange("p k d -> p (k d)"),
                       (I32, J32)[q][:]).then_inc(xT_ps, 1)
            pe.wait_ge(iwk_ready, 1)
            for q in range(2):
                for r in range(3):
                    for k in range(2):
                        o = (2 * r + k) * P
                        t.transpose(PS[:, 4 + 2 * q + o // 512, o % 512:o % 512 + P],
                                    iwk[:, q, r, 2 * k:2 * k + 2].rearrange("p k d -> p (k d)"), I32[:])
                t.transpose(PS[0:HD, 5 + 2 * q, 2 * P:3 * P], iw[:, q, 0], I32[:])
                last = t.transpose(PS[0:HD, 5 + 2 * q, 3 * P:3 * P + 2], iwdt[0:2, q], I32[0:2, 0:2])
            last.then_inc(w_ps, 1)
            pe.wait_ge(xT_a, 2)
            pe.wait_ge(xT_v, 2)
            pe.wait_ge(w_sb, 2)
            for q in range(2):
                for c in range(TC):
                    o = 2 * (q * TC + c)
                    last = mm(PS[:, 0, o:o + 2], xT2[0:HD, q, 3 + c * P:3 + (c + 1) * P], WdT[0:HD, q])
            last.then_inc(dt_ps, 1)

            pe.wait_ge(ld_mw, N_MW)
            t.transpose(PS[:, 3, 0:P], opw, I32[:]).then_inc(op_ps, 1)
            pe.wait_ge(op_sb, 1)
            for q in range(2):
                r = slice(HD * q, HD * q + HD)
                last = mm(PS[:, 1 + q, 0:P], ow[r, :], opT[r, :])
            last.then_inc(op_ps, 1)
            pe.wait_ge(op_sb, 3)
            pe.wait_ge(dt_v, 1)
            def convolve(c):
                for q in range(2):
                    b0 = PS[:, 4 * q]
                    after(pe, silu_done[q], 4 * c)
                    mm(b0[:, 0:P], WzT[0:HD, q], xT2[0:HD, q, bass.ds(c * P + 3, P)])
                    for r in range(3):
                        for k in range(2):
                            last = mm(b0[:, (r + 1) * P:(r + 2) * P], WcT[:, q, r, k],
                                      xT2[:, q, bass.ds(c * P + 2 * k, P)], start=k == 0, stop=k == 1)
                    last.then_inc(conv_done[q], 1)

            def chunk_pe(c, last_one=False):
                for q in range(2):
                    b1 = PS[:, 4 * q + 1]
                    after(pe, b1_read[q], c)
                    pe.wait_ge(dg_ready[q], c + 1)
                    mm(b1[:, 2 * P:4 * P], ones[:], dg[:, q].rearrange("p h n -> p (h n)"))
                    pe.wait_ge(silu_done[q], 4 * c + 4)
                    t.transpose(b1[:, 0:P], xc[:, q], I32[:])
                    t.transpose(b1[:, P:2 * P], Bc[:, q], I32[:]).then_inc(t_done[q], 1)
                    after(pe, h_done[q], c)
                    mm(PS[:, 4 * q + 2, 0:P], Bc[:, q], Cc[:, q]).then_inc(g_done[q], 1)
                if not last_one:
                    convolve(c + 1)
                for q in range(2):
                    pe.wait_ge(m_done[q], c + 1)
                    pe.wait_ge(xw_done[q], c + 1)
                    mm(PS[:, 4 * q + 2, P:2 * P], Bm[:, q], Xw[:, q]).then_inc(s_done[q], 1)
                    pe.wait_ge(cdec_ready[q], c + 1)
                    after(pe, out_evac[q], c)
                    for k, (l, r) in enumerate(((Xp, Mt), (Hp, CD))):
                        for h in range(2):
                            last = mm(PS[:, 4 * q + 3, 0:P], l[:, q, h * P:(h + 1) * P], r[:, q, h],
                                      start=k + h == 0, stop=k + h == 2)
                    last.then_inc(y_done[q], 1)
                for q in range(2):
                    pe.wait_ge(yg_done[q], c + 1)
                    mm(PS[:, 4 * q + 3, P:2 * P], yg[:, q], Wout[:, q])
                    pe.wait_ge(sq_done[q], c + 1)
                    mm(PS[:, 4 * q + 3, 2 * P:2 * P + 1], sq[:, q], ones[:, 0:1]).then_inc(out_done[q], 1)

            convolve(0)
            chunk_pe(0)
            with pe.Fori(1, TC - 1) as c:
                chunk_pe(c)
            chunk_pe(TC - 1, last_one=True)
            def turn_round():
                pe.wait_ge(yo_ready, 1)
                for i in range(2):
                    mm(PS[:, i, :], J32[:], yo[:, 1, 4 * i:4 * i + 4, 0:D]).then_inc(J_ps, 1)

            for q in range(2):
                pe.wait_ge(out_evac[q], TC)
                pe.wait_ge(h_done[q], TC)
            pe.wait_ge(t_ready, 3)
            pe.wait_ge(bsel_ready, 1)
            pe.wait_ge(ld_b, 48)

            def projected(h):
                hs = slice(h * D, (h + 1) * D)
                if h > EARLY:
                    pe.wait_ge(ah_sb, 2 * h)
                elif h >= 2:
                    pe.wait_ge(wt_sb, 2 * h - 2)
                b0, b1 = (PS[:, b] for b in W_BANKS(h)[0:2])
                both = Tm[:].rearrange("p g d -> p (g d)")
                mm(b0[:, 0:P], Wq[:, hs], Tm[:, 1], stop=False)
                mm(b0[:, 0:P], brow[0:3, hs], bsel[0:3, 0, 0], start=False)
                mm(b0[:, P:3 * P], Wkv[:, hs], both, stop=False)
                mm(b0[:, P:3 * P], brow[0:3, hs], bsel[0:3, 1].rearrange("p g n -> p (g n)"), start=False).then_inc(wt_ps, 1)
                mm(b1[:, 0:2 * P], Wkv[:, H * D + h * D:H * D + (h + 1) * D], both, stop=False)
                mm(b1[:, 0:2 * P], brow[0:3, hs], bsel[0:3, 2].rearrange("p g n -> p (g n)"), start=False).then_inc(wt_ps, 1)

            def combined(h):
                k = h % 2
                pe.wait_ge(wt_sb, 2 * h + 2)
                if 2 <= h < EARLY:
                    pe.wait_ge(ah_sb, 2 * h - 2)
                bank, w = PS[:, W_BANKS(h)[2]], WT[:, h % 2]
                mm(bank[:, 0:2 * P], w[:, 0:P], w[:, P:3 * P])
                for g in range(2):
                    last = mm(bank[:, (2 + g) * P:(3 + g) * P], w[:, (3 + g) * P:(4 + g) * P], Wo[:, h])
                last.then_inc(ah_ps, 1)

            projected(0)
            turn_round()
            for h in range(1, EARLY):
                projected(h)
                combined(h - 1)
            combined(EARLY - 1)

            def latents_pe():
                pe.wait_ge(z_ones, 1)
                for c in range(TC):
                    t.transpose(PS[:, c // 4, c % 4 * P:(c % 4 + 1) * P], x_sb[:, c, :], I32[:]).then_inc(zlT_ps, 1)

            for i, (c0, w) in enumerate(KV_GROUPS + [(0, 1)]):
                if i == LAT_AT:
                    latents_pe()
                for src, s_rdy, s_free, o in ((Zhi, z_hi, zt_hi, 0), (Zlo, z_lo, zt_lo, 1)):
                    if i == 0:
                        pe.wait_ge(s_rdy, N_HI)
                    if i >= DVE_AT + 2 and o == 1:
                        pe.wait_ge(zt_lo_v, i - 1 - DVE_AT)
                    elif i >= 2:
                        pe.wait_ge(s_free, i - 1)
                    elif o == 0:
                        pe.wait_ge(wt_sb, 2 * EARLY)
                    for k in range(w):
                        n = P if c0 else LEFT
                        last = mm(PS[:, 2 + 2 * (i % 2) + o, k * P:k * P + n], src[0:n, c0 + k, :], I16[0:n, 0:n])
                    last.then_inc(zt_ps, 1)

            def scores(j, st, ring, i):
                g, (r, turn) = step_number(j, st), place_of(st)
                if i >= len(STEPS[r]):
                    return
                if i == 0:
                    if not early(j, st, 2):
                        pe.wait_ge(p32_ready, g - 1)
                    if r == 0:
                        pe.wait_ge(row_lo, j + 1)
                ch = STEPS[r][i]
                o = PS[:, 2 * (r % 2) + i, :]
                k = 2 if is_latent(ch) else 0
                zh, zl = (z[:, bass.ds(turn * (12 * P) + ch * P, P)] for z in (ZThi, ZTlo))
                mm(o, zh, A[:, ring, k, :], stop=False)
                mm(o, zh, A[:, ring, k + 1, :], start=False, stop=False)
                last = mm(o, zl, A[:, ring, k, :], start=False)
                if i == len(STEPS[r]) - 1:
                    last.then_inc(qk_done, 1)

            def sums(r, turn, i):
                ch = STEPS[r][i]
                latent = is_latent(ch)
                return (PS[:, 5 if latent else 4, :], ch == (LAT0 if latent else 0),
                        ch == (CTX0 - 1 if latent else NCH - 1), Zhi[:, turn * 12 + ch, :], Zlo[:, turn * 12 + ch, :])

            def values_high(g, r, turn=0):
                pe.wait_ge(hi_ready, g + 1)
                for i in range(len(STEPS[r])):
                    o, first, _, zh, zl = sums(r, turn, i)
                    p = Phi[:, r % 3, i * QB:(i + 1) * QB]
                    mm(o, zh, p, start=first, stop=False)
                    mm(o, zl, p, start=False, stop=False)

            def values_low(g, r, turn=0):
                pe.wait_ge(lo_ready, g + 1)
                for i in range(len(STEPS[r])):
                    o, _, end, zh, _ = sums(r, turn, i)
                    last = mm(o, zh, Plo[:, r % 3, i * QB:(i + 1) * QB], start=False, stop=end)
                last.then_inc(pv_done, 1)

            def unit(n, par, kb, i, ring):
                if not (isinstance(n, int) and n < 2):
                    pe.wait_ge(mx_read, n - 1)
                unit_product(PS[:, 6 + par], kb, i, ring)

            def unit_product(bank, kb, i, ring):
                static = isinstance(kb, int)
                latent = static and kb >= KB_LAT
                w = 2 * P if static and kb == KB_LEFT else QB
                at = LAT0 * P + (kb - KB_LAT) * QB if latent else kb * QB + CTX0 * P
                q = A[:, ring, 2 if latent else 0, i * P:(i + 1) * P]
                last = mm(bank[:, 0:w], q, ZThi[:, bass.ds(at, w)])
                if w < QB:
                    last = mm(bank[:, w:w + LEFT], q, ZThi[:, 0:LEFT])
                last.then_inc(mx_done, 1)

            def max_to_row(b):
                pe.wait_ge(m_neg, b + 1)
                for i in range(4):
                    last = mm(PS[0:1, 6, i * P:(i + 1) * P], mcol[:, 1, i:i + 1], I32[:])
                last.then_inc(m_row, 1)

            def project(b, k):
                pe.wait_ge(u_evac, b + 1)
                for i in range(2):
                    for g in range(2):
                        at = (2 * k + i) * P
                        last = mm(PS[:, 7 - k, 256 * i:256 * i + D + 2], U_sb[:, g, at:at + P], VO[:, b % H, g, :],
                                  start=g == 0, stop=g == 1)
                last.then_inc(o_ps, 1)

            def slots(units):
                return (units[0:1], units[1:2], units[2:3]) if len(units) == 3 else (units[0:1], [], units[1:2])

            def block_pe(j, first=False, maxes=True, nxt=True):
                b = j + 1
                ring, nring = j % 4, (j + 1) % 4
                u = 0
                for st in range(LOOP0):
                    units = list(range(u, u + UNITS_HEAD[st])) if maxes else []
                    u += UNITS_HEAD[st]
                    s0, s1, s2 = slots(units)
                    lag = st - 2 if st >= 2 else NS + st - 2
                    lagged = NS * j + st - 2 if st >= 2 or not first else None

                    def some(us):
                        for w in us:
                            unit(NU * b + w, w % 2, KB_LEFT + w // 4, w % 4, nring)

                    scores(j, st, ring, 0)
                    if st == 1 and maxes:
                        pe.wait_ge(a_lo, 2 * b + 2)
                    some(s0)
                    scores(j, st, ring, 1)
                    some(s1)
                    if lagged is not None:
                        if st == 2 and not first:
                            pe.wait_ge(u_evac, j)
                        values_high(lagged, lag)
                    some(s2)
                    if lagged is not None:
                        values_low(lagged, lag)
                with pe.Fori(0, LOOPN) as i:
                    u = 0
                    for k in range(6):
                        units = list(range(u, u + UNITS_TURN[k])) if maxes else []
                        u += UNITS_TURN[k]
                        s0, s1, s2 = slots(units)
                        lagged, lag = NS * j + 6 * i + (LOOP0 + k - 2), LOOP0 + k - 2

                        def some(us):
                            for w in us:
                                unit(NU * b + 16 * i + (12 + w), w % 2, 4 * i + w // 4, w % 4, nring)

                        scores(j, Turn(i, k), ring, 0)
                        some(s0)
                        scores(j, Turn(i, k), ring, 1)
                        some(s1)
                        values_high(lagged, lag, i)
                        some(s2)
                        values_low(lagged, lag, i)
                for st in range(TAIL, NS):
                    scores(j, st, ring, 0)
                    scores(j, st, ring, 1)
                    if st == TAIL + 1 and maxes:
                        max_to_row(b)
                    if st == TAIL + 2 and not first:
                        project(j - 1, 0)
                    if st == TAIL + 3:
                        if maxes:
                            pe.wait_ge(row_sum, b + 1)
                        if not first:
                            project(j - 1, 1)
                    values_high(NS * j + (st - 2), st - 2)
                    values_low(NS * j + (st - 2), st - 2)
                    if st == TAIL + 3 and nxt:
                        if not first:
                            pe.wait_ge(o_acc, 2 * j)
                        a_side(j + 2)

            def a_side(b):
                zh, zl = (z[:, bass.ds((b // H) * QB + LAT0 * P, QB)] for z in (ZThi, ZTlo))
                for g in range(2):
                    mm(PS[:, 7 - g, :], AHhi[:, b % H, g], zh, stop=False)
                    mm(PS[:, 7 - g, :], AHhi[:, b % H, g], zl, start=False, stop=False)
                    mm(PS[:, 7 - g, :], AHlo[:, b % H, g], zh, start=False).then_inc(a_ps, 1)

            pe.wait_ge(zlT_a, 2)
            pe.wait_ge(zlT_v, 2)
            pe.wait_ge(ah_sb, 2 * EARLY)
            pe.wait_ge(ah_lo, 1)
            a_side(0)
            pe.wait_ge(zt_hi, len(KV_GROUPS) + 1)
            pe.wait_ge(zt_lo, DVE_AT)
            pe.wait_ge(zt_lo_v, len(KV_GROUPS) + 1 - DVE_AT)
            pe.wait_ge(z_lo, N_HI + 1)
            pe.wait_ge(a_lo, 2)

            for n in range(NU // 2):
                if n >= 3:
                    pe.wait_ge(mx_read, 2 * n - 4)
                for i in range(2):
                    unit_product(PS[:, n % 3 * 2 + i], n // 2, n % 2 * 2 + i, 0)
                if 4 <= n < 4 + 4 * (H - EARLY):
                    h = EARLY + (n - 4) // 4
                    if n % 4 == 0:
                        projected(h)
                    elif n % 4 == 2:
                        combined(h)
                if n == 21:
                    pe.wait_ge(ah_sb, 2 * H)
                    pe.wait_ge(ah_lo, H)
                    a_side(1)
            max_to_row(0)
            block_pe(0, first=True)
            with pe.Fori(1, NBLK - 2) as j:
                block_pe(j)
            block_pe(NBLK - 2, nxt=False)
            block_pe(NBLK - 1, maxes=False, nxt=False)
            for r in (NS - 2, NS - 1):
                values_high(NS * (NBLK - 1) + r, r)
                values_low(NS * (NBLK - 1) + r, r)
            pe.wait_ge(o_acc, 2 * (NBLK - 1))
            project(NBLK - 1, 0)
            project(NBLK - 1, 1)

            pe.wait_ge(xf_ready, 1)
            for c in range(TC):
                t.transpose(PS[:, c // 4, c % 4 * P:(c % 4 + 1) * P], xf[:, c, :], I32[:]).then_inc(xfT_ps, 1)
            pe.wait_ge(xfT_v, 2)
            for c in range(TC):
                last = mm(PS[:, 2, c * E:(c + 1) * E], xfT[:, c * P:(c + 1) * P], rw[:])
            last.then_inc(rt_ps, 1)
            pe.wait_ge(xf_hi, 1)
            pe.wait_ge(xf_lo, 1)
            pe.wait_ge(rt_v, 1)

            def gate_up(u, k, hi, lo, at, o, half):
                if o == 0 and not (isinstance(u, int) and u < 2):
                    pe.wait_ge(f_clip, u - 1)
                if o == 1 and not (isinstance(u, int) and u < RING):
                    pe.wait_ge(f_hid, u + (1 - RING))
                xh, xl = (x[:, half * QB:(half + 1) * QB] for x in (xfhi, xflo))
                bank, c = PS[:, 2 + k % RING if o else k % 2], slice(at, at + P)
                mm(bank, hi[:, c], xh, stop=False)
                mm(bank, hi[:, c], xl, start=False, stop=False)
                mm(bank, lo[:, c], xh, start=False).then_inc((f_gate, f_up)[o], 1)

            def down(n, n_low, half, c, his, los):
                pe.wait_ge(f_lo, n_low)
                if not (isinstance(n, int) and n < 2):
                    pe.wait_ge(dn_acc, n - 1)
                o = PS[:, 6 + c % 2, 0:P]
                for i in range(len(his)):
                    hh, hl = (h[:, half, i, c * P:(c + 1) * P] for h in (hhi, hlo))
                    mm(o, hh, his[i], start=i == 0, stop=False)
                    mm(o, hh, los[i], start=False, stop=False)
                    last = mm(o, hl, his[i], start=False, stop=i == len(his) - 1)
                last.then_inc(dn_ps, 1)

            def routed_down(e, m):
                down(8 * e + m, 8 * e + (4 * (m // 4) + 4), m // 4, m % 4,
                     [DNhi[:, e, i, :] for i in range(4)], [DNlo[:, e, i, :] for i in range(4)])

            def expert_pe(e, first=False):
                pe.wait_ge(stage_used, NPART * e + NPART)
                for k in range(8):
                    for o in range(2):
                        gate_up(8 * e + k, k, GUhi[:, e], GUlo[:, e], k % 4 * P + F * o, o, k // 4)
                        for m in TILES[k][o]:
                            if m < 2 or not first:
                                routed_down(e if m < 2 else e - 1, m)

            expert_pe(0, first=True)
            with pe.Fori(1, E) as e:
                expert_pe(e)
            pe.wait_ge(stage_used, NPART * E + 2)
            for half in range(2):
                for o in range(2):
                    gate_up(8 * E + half, half, SGhi, SGlo, FS * o, o, half)
                    if half == 0:
                        routed_down(E - 1, 2 + o)
            for m in range(4, 8):
                routed_down(E - 1, m)
            for m in range(8):
                down(8 * E + m, 8 * E + m // 4 + 1, m // 4, m % 4, [SDhi], [SDlo])


_NAMES = {
    "x": "x", "ctx_1024": "ctx", "L0_attn_norm_w": "norm_w", "L0_attn_op_w": "op_w", "L0_attn_op_b": "op_b",
    "L0_xattn_gamma_media": "gamma_media", "L0_xattn_beta_media": "beta_media", "L0_xattn_gamma_lat": "gamma_lat",
    "L0_xattn_beta_lat": "beta_lat", "L0_xattn_Wq": "Wq", "L0_xattn_bq": "bq", "L0_xattn_Wkv": "Wkv",
    "L0_xattn_bkv": "bkv", "L0_xattn_Wo": "Wo", "L0_xattn_bo": "bo", "L0_ffn_ln_gamma": "ln_gamma",
    "L0_ffn_ln_beta": "ln_beta", "L0_ffn_router_w": "router_w", "L0_ffn_gate_up_w": "gate_up_w",
    "L0_ffn_down_w": "down_w", "L0_ffn_shared_gate_up_w": "shared_gate_up_w", "L0_ffn_shared_down_w": "shared_down_w",
}
_MAMBA = ["in_w", "conv_w", "conv_b", "dt_bias", "A_log", "D", "gnorm_w", "outp_w"]


def kernel(**inputs):
    import numpy as _np
    import concourse.bacc as _bacc
    from concourse.bass_utils import run_bass_kernel_spmd as _run

    nc = _bacc.Bacc("TRN2", target_bir_lowering=False, num_devices=1)
    arrays = {}

    def dram(name):
        x = _np.ascontiguousarray(inputs[name])
        arrays[f"in_{name}"] = x
        return nc.dram_tensor(f"in_{name}", x.shape, mybir.dt.from_np(x.dtype), kind="ExternalInput").ap()

    a = {short: dram(name) for name, short in _NAMES.items()}
    for q in "fb":
        a[q] = {m: dram(f"L0_attn_{q}_{m}") for m in _MAMBA}
    out = nc.dram_tensor("out_0", (1, T, D), F32, kind="ExternalOutput").ap()
    layer(nc, a, out)
    return _run(nc, [arrays], core_ids=[0]).results[0]["out_0"]
```
